# Optimizing a Trainium2 kernel written in Bass

```python
import numpy as np
import jax
import jax.numpy as jnp

def _softmax(x, axis=-1):
    return jax.nn.softmax(x, axis=axis)

def _gelu(x):
    return jax.nn.gelu(x, approximate=True)

def _silu(x):
    return jax.nn.silu(x)

def _sigmoid(x):
    return jax.nn.sigmoid(x)

def _layernorm(x, axis=-1, eps=1e-05):
    m = jnp.mean(x, axis=axis, keepdims=True)
    v = jnp.var(x, axis=axis, keepdims=True)
    return (x - m) / jnp.sqrt(v + eps)

def _scatter_add(tgt, idx, src, axis=0):
    return tgt.at[idx].add(src)

def _segment_sum(src, seg, n):
    return jax.ops.segment_sum(src, seg, n)
kernel_name = 'mk_adj_preln_d2_adj_r2_410171'

def setup_inputs(seed: int=0):
    np.random.seed(seed)
    _w = jnp.asarray

    def _rec_inputs():
        import jax
        import jax.numpy as jnp
        _gk = jax.random.key(seed)
        x = -0.0003929 + 0.9999 * jax.random.normal(jax.random.fold_in(_gk, 1), (8, 1024, 256), jnp.float32)
        _a = jax.random.bernoulli(jax.random.fold_in(_gk, 2), 0.00195312, (8, 1024, 1024))
        _a = jnp.logical_or(_a, jnp.swapaxes(_a, -1, -2))
        _a = jnp.logical_or(_a, jnp.eye(1024, dtype=bool))
        _af = _a.astype(jnp.float32)
        _af = _af * jax.random.uniform(jax.random.fold_in(_gk, 3), (8, 1024, 1024), jnp.float32, 0.05, 1)
        adj = _af
        return (x, adj)
    x, adj = _rec_inputs()

    def _L0_gnn_setup():
        import jax, jax.numpy as jnp
        import numpy as np
        B, N, C_IN, C_OUT = (8, 2048, 256, 256)
        key = jax.random.key(seed)
        k1, k2, k3, k4 = jax.random.split(key, 4)
        node_features = jax.random.normal(k1, (B, N, C_IN), dtype=jnp.float32)
        adj_matrix = jax.random.uniform(k2, (B, N, N), dtype=jnp.float32)
        W = jax.random.normal(k3, (C_IN, C_OUT), dtype=jnp.float32) / np.sqrt(C_IN)
        b = jax.random.normal(k4, (C_OUT,), dtype=jnp.float32) * 0.01
        return {'node_features': node_features, 'adj_matrix': adj_matrix, 'W': W, 'b': b}
    _L0_gnn_all = _L0_gnn_setup()
    _L0_gnn_in = {k: v for k, v in _L0_gnn_all.items() if k in ('W', 'b')}
    del _L0_gnn_all

    def _L1_gnn_setup():
        import jax, jax.numpy as jnp
        import numpy as np
        B, N, D = (8, 1024, 256)
        key = jax.random.key(seed)
        ks = jax.random.split(key, 8)
        scale = 0.5 / np.sqrt(D)
        x = jax.random.normal(ks[0], (B, N, D), dtype=jnp.float32)
        adj = jax.random.uniform(ks[1], (B, N, N), dtype=jnp.float32)
        Wq_w = jax.random.normal(ks[2], (D, D), dtype=jnp.float32) * scale
        Wk_w = jax.random.normal(ks[3], (D, D), dtype=jnp.float32) * scale
        Wv_w = jax.random.normal(ks[4], (D, D), dtype=jnp.float32) * scale
        Wq_b = jnp.zeros((D,), dtype=jnp.float32)
        Wk_b = jnp.zeros((D,), dtype=jnp.float32)
        Wv_b = jnp.zeros((D,), dtype=jnp.float32)
        return {'x': x, 'adj': adj, 'Wq_w': Wq_w, 'Wq_b': Wq_b, 'Wk_w': Wk_w, 'Wk_b': Wk_b, 'Wv_w': Wv_w, 'Wv_b': Wv_b}
    _L1_gnn_all = _L1_gnn_setup()
    _L1_gnn_in = {k: v for k, v in _L1_gnn_all.items() if k in ('Wq_w', 'Wq_b', 'Wk_w', 'Wk_b', 'Wv_w', 'Wv_b')}
    del _L1_gnn_all
    return {'x': x, 'adj': adj, 'L0_gnn_W': _L0_gnn_in['W'], 'L0_gnn_b': _L0_gnn_in['b'], 'L1_gnn_Wq_w': _L1_gnn_in['Wq_w'], 'L1_gnn_Wq_b': _L1_gnn_in['Wq_b'], 'L1_gnn_Wk_w': _L1_gnn_in['Wk_w'], 'L1_gnn_Wk_b': _L1_gnn_in['Wk_b'], 'L1_gnn_Wv_w': _L1_gnn_in['Wv_w'], 'L1_gnn_Wv_b': _L1_gnn_in['Wv_b']}

def reference(x, adj, L0_gnn_W, L0_gnn_b, L1_gnn_Wq_w, L1_gnn_Wq_b, L1_gnn_Wk_w, L1_gnn_Wk_b, L1_gnn_Wv_w, L1_gnn_Wv_b):
    import jax
    import jax.numpy as jnp

    def _L0_gnn_ref(node_features, adj_matrix, W, b):
        import jax, jax.numpy as jnp
        import numpy as np
        B, N, C_IN, C_OUT = (8, 2048, 256, 256)
        num_neighbours = adj_matrix.sum(axis=-1, keepdims=True)
        h = jnp.einsum('bni,io->bno', node_features, W) + b
        h = jnp.einsum('bnm,bmo->bno', adj_matrix, h)
        return h / num_neighbours

    def _L1_gnn_ref(x, adj, Wq_w, Wq_b, Wk_w, Wk_b, Wv_w, Wv_b):
        import jax, jax.numpy as jnp
        import numpy as np
        B, N, D = (8, 1024, 256)
        query = jnp.einsum('bnd,od->bno', x, Wq_w) + Wq_b
        keyt = jnp.einsum('bnd,od->bno', x, Wk_w) + Wk_b
        value = jnp.einsum('bnd,od->bno', x, Wv_w) + Wv_b
        weight = jnp.einsum('bqd,bkd->bqk', query, keyt)
        weight = adj * jnp.exp(weight)
        weight = weight / jnp.sum(weight, axis=2, keepdims=True)
        return jnp.einsum('bqk,bkd->bqd', weight, value)
    h = jnp.maximum(_layernorm(x, axis=-1), 0.0)
    x = x + _L0_gnn_ref(h, adj, L0_gnn_W, L0_gnn_b)
    h = jnp.maximum(_layernorm(x, axis=-1), 0.0)
    x = x + _L1_gnn_ref(h, adj, L1_gnn_Wq_w, L1_gnn_Wq_b, L1_gnn_Wk_w, L1_gnn_Wk_b, L1_gnn_Wv_w, L1_gnn_Wv_b)
    return x

_drawn_inputs = setup_inputs


def setup_inputs(seed=0):
    import zlib

    import numpy as np

    out = dict(_drawn_inputs(seed))
    spreads = {'L1_gnn_Wq_b': (0.0, 0.1), 'L1_gnn_Wk_b': (0.0, 0.8), 'L1_gnn_Wv_b': (0.0, 0.1)}
    factors = {'L0_gnn_b': 6.888}
    for name, (base, spread) in spreads.items():
        noise = np.random.default_rng([zlib.crc32(name.encode()), seed]).standard_normal(out[name].shape)
        drawn = base * np.exp(spread * noise) if base else spread * noise
        out[name] = jnp.asarray(drawn.astype(out[name].dtype))
    for name, factor in factors.items():
        out[name] = (out[name] * factor).astype(out[name].dtype)
    return out
```

```python
import concourse.bass as bass
from concourse import mybir
from contextlib import ExitStack

F32 = mybir.dt.float32
F32R = mybir.dt.float32r
ALU = mybir.AluOpType
ACT = mybir.ActivationFunctionType
AX = mybir.AxisListType

P = 128
EPS = 1e-5


def build(nc, x, adj, w0, b0, wq, bq, wk, bk, wv, bv, out):
    B, N, C = x.shape
    CH = C // P
    Q = 512
    NC = N // Q
    KT = N // P
    QT = Q // P
    TILES = NC * KT
    MH = N // Q
    VW = C + 2
    assert (CH, NC, KT, QT, TILES, MH) == (2, 2, 8, 4, 16, 2)
    LOOPS = B - 2

    adj_v = adj.rearrange("b (c r p) (h m) -> b c h p r m", c=NC, p=P, h=MH)
    x_v = x.rearrange("b (r p) d -> b p r d", p=P)
    out_v = out.rearrange("b (c r p) d -> b c p r d", c=NC, p=P)

    with ExitStack() as ctx:
        def sb(name, shape, dt=F32):
            return ctx.enter_context(nc.sbuf_tensor(name, shape, dt))

        def ps(name, shape):
            return ctx.enter_context(nc.psum_tensor(name, shape, F32))

        def sem(name):
            return ctx.enter_context(nc.semaphore(name))

        rows = sb("rows", [P, MH, QT, Q])
        a_t = sb("a_t", [P, NC, KT, Q])
        a_hi = sb("a_hi", [P, 2, Q], F32R)
        a_lo = sb("a_lo", [P, 2, Q], F32R)
        x_in = sb("x_in", [P, KT, C])
        xb = sb("xb", [P, KT, C])
        hf = sb("hf", [P, 2, C])
        h0_hi = sb("h0_hi", [P, KT, C], F32R)
        h0_lo = sb("h0_lo", [P, KT, C], F32R)
        g_hi = sb("g_hi", [P, CH, Q], F32R)
        g_lo = sb("g_lo", [P, CH, Q], F32R)
        scrap = sb("scrap", [P, Q])
        rsum = sb("rsum", [P, MH, QT])
        rsum2 = sb("rsum2", [P, QT])
        rinv0 = sb("rinv0", [P, QT])
        x1 = sb("x1", [P, KT, C])
        h1 = sb("h1", [P, QT, C])
        ht_hi = sb("ht_hi", [P, CH, N], F32R)
        ht_lo = sb("ht_lo", [P, CH, N], F32R)
        z_hi = sb("z_hi", [P, CH, N], F32R)
        z_lo = sb("z_lo", [P, CH, N], F32R)
        v_hi = sb("v_hi", [P, KT, VW], F32R)
        v_lo = sb("v_lo", [P, KT, C], F32R)
        gk = sb("gk", [P, KT])
        pf = sb("pf", [P, Q])
        p_hi = sb("p_hi", [P, 2, Q], F32R)
        p_lo = sb("p_lo", [P, 2, Q], F32R)
        rinv1 = sb("rinv1", [P, QT])
        o_sb = sb("o_sb", [P, QT, C])
        st0 = sb("st0", [P, QT, 6])
        mv0 = sb("mv0", [P, NC, QT, 2])
        ve0 = sb("ve0", [P, NC, QT])
        nm0 = sb("nm0", [P, NC, QT])
        rstd0 = sb("rstd0", [P, NC, QT])
        nmr0 = sb("nmr0", [P, NC, QT])
        st1 = sb("st1", [P, 2, 6])
        mv1 = sb("mv1", [P, 2, 2, 2])
        ve1 = sb("ve1", [P, 2, 2])
        nm1 = sb("nm1", [P, 2, 2])
        rstd1 = sb("rstd1", [P, 2, 2])
        nmr1 = sb("nmr1", [P, 2, 2])
        ident = sb("ident", [P, P])
        ones = sb("ones", [P, P])
        mhalf = sb("mhalf", [P, QT])
        w_hi = sb("w_hi", [P, CH, C], F32R)
        w_lo = sb("w_lo", [P, CH, C], F32R)
        m_hi = sb("m_hi", [P, CH, C], F32R)
        m_lo = sb("m_lo", [P, CH, C], F32R)
        wv_hi = sb("wv_hi", [P, CH, VW], F32R)
        wv_lo = sb("wv_lo", [P, CH, VW], F32R)
        b0_all = sb("b0_all", [P, C])
        bv_all = sb("bv_all", [P, C])
        bqk = sb("bqk", [P, 2, CH])
        bprod = sb("bprod", [P, CH])
        bz = sb("bz", [P, CH])
        s0 = sb("s0", [P, 1])
        w_f = x1[:, 0:CH, :]
        wq_f = x1[:, CH:2 * CH, :]
        wk_f = x1[:, 2 * CH:3 * CH, :]
        wv_f = x1[:, 3 * CH:4 * CH, :]

        bank_t = ps("bank_t", [P, Q])
        bank_s = ps("bank_s", [P, Q])
        agg = ps("agg", [P, CH, Q])
        att = ps("att", [P, QT, Q])

        rows_in = [sem(f"rows_in{h}") for h in range(MH)]
        x_got = sem("x_got")
        weights_in = sem("weights_in")
        biases_in = sem("biases_in")
        stored = sem("stored")
        ident_zero = sem("ident_zero")
        ident_ready = sem("ident_ready")
        bprod_ready = sem("bprod_ready")
        setup_pe = sem("setup_pe")
        setup_dve = sem("setup_dve")
        weights_ready = sem("weights_ready")
        tr_done = sem("tr_done")
        ah_done = sem("ah_done")
        y_done = sem("y_done")
        ht_done = sem("ht_done")
        z_done = sem("z_done")
        v_done = sem("v_done")
        s_done = sem("s_done")
        pv_done = sem("pv_done")
        a_hi_ready = sem("a_hi_ready")
        a_t_ready = sem("a_t_ready")
        rsum_ready = sem("rsum_ready")
        exp_ready = sem("exp_ready")
        g_hi_ready = sem("g_hi_ready")
        ht_hi_ready = sem("ht_hi_ready")
        z_hi_ready = sem("z_hi_ready")
        v_hi_ready = sem("v_hi_ready")
        hf_ready = sem("hf_ready")
        h1_ready = sem("h1_ready")
        a_lo_ready = sem("a_lo_ready")
        p_ready = sem("p_ready")
        p_hi_ready = sem("p_hi_ready")
        p_lo_ready = sem("p_lo_ready")
        g_lo_ready = sem("g_lo_ready")
        rsum2_ready = sem("rsum2_ready")
        rinv0_ready = sem("rinv0_ready")
        ht_lo_ready = sem("ht_lo_ready")
        z_lo_ready = sem("z_lo_ready")
        v_lo_ready = sem("v_lo_ready")
        gk_ready = sem("gk_ready")
        h0_hi_ready = sem("h0_hi_ready")
        h0_ready = sem("h0_ready")
        x1_ready = sem("x1_ready")
        x1_tile = sem("x1_tile")
        bn0 = sem("bn0")
        mv0_ready = sem("mv0_ready")
        st0_ready = sem("st0_ready")
        bn1 = sem("bn1")
        mv1_ready = sem("mv1_ready")
        st1_ready = sem("st1_ready")
        rinv1_ready = sem("rinv1_ready")
        out_ready = sem("out_ready")
        pow0 = sem("pow0")
        ln0_ready = sem("ln0_ready")
        pow1 = sem("pow1")
        ln1_ready = sem("ln1_ready")
        xb_ready = sem("xb_ready")
        x1b_ready = sem("x1b_ready")

        def nth(per, batch, n, by=1):
            value = (batch * per + (n + 1)) * by
            return max(value, 0) if isinstance(value, int) else value

        def turns(eng, step, setup):
            setup()
            for s in range(TILES):
                step(-1, s, False, True, True, False)
            step(0, 0, True, True, True, False)
            with eng.Fori(0, LOOPS) as i:
                for s in range(1, TILES):
                    step(i, s, True, True, True, True)
                step(i + 1, 0, True, True, True, True)
            for s in range(1, TILES):
                step(B - 2, s, True, True, False, True)
            step(B - 1, 0, True, False, False, True)
            for s in range(1, TILES):
                step(B - 1, s, True, False, False, True)
            step(B, 0, False, False, False, True)

        def norm_steps(i, s, layer1, layer0):
            if s in (1, 2) and layer1:
                return i, 1, s - 1
            if s in (9, 10) and layer0:
                return i + 1, 0, s - 9
            return None

        def relu_steps(i, s, layer1, layer0):
            return norm_steps(i, s - 1, layer1, layer0)

        def prep_steps(i, s, layer1, layer0):
            if s == 4 and layer1:
                return i, 1
            if s == 12 and layer0:
                return i + 1, 0
            return None

        def h0_steps(i, s, layer0, after):
            if 10 <= s and after:
                return i + 2, s - 10
            if s < 2 and layer0:
                return i + 1, 6 + s
            return None

        block = ctx.enter_context(nc.Block())

        @block.sync
        def _(sp):
            def load_rows(a, c, h):
                sp.dma_start(rows[:, h], adj_v[a, c, h]).then_inc(rows_in[h], 16)

            def load_x(a):
                sp.dma_start(x_in[:, :, :], x_v[a]).then_inc(x_got, 16)

            def setup():
                sp.sem_inc(stored, 16)
                load_x(0)
                load_rows(0, 0, 0)
                load_rows(0, 0, 1)

            def step(i, s, layer1, layer0, after, before):
                b, a = i, i + 1
                c, t = s // KT, s % KT
                if s == 4 and after:
                    sp.wait_ge(xb_ready, nth(NC, a, 1))
                    sp.wait_ge(hf_ready, nth(KT, a, KT - 1))
                    load_x(a + 1)
                if t in (3, 7) and (layer0 if c == 0 else after):
                    sp.wait_ge(tr_done, nth(TILES, a, s))
                    sp.wait_ge(rsum_ready, nth(TILES, a, s))
                    load_rows(a + c, 1 - c, t // QT)
                if t == 0 and (before if c == 0 else layer1):
                    ob = b - 1 if c == 0 else b
                    sp.wait_ge(out_ready, nth(NC, ob, 2 - c))
                    sp.dma_start(out_v[ob, 1 - c], o_sb[:, :, :]).then_inc(stored, 16)

            turns(sp, step, setup)
            sp.wait_ge(stored, nth(NC, B - 1, NC, 16))

        @block.gpsimd
        def _(pool):
            def add_b0(a, c):
                pool.wait_ge(x_got, nth(1, a, 0, 16))
                pool.wait_ge(x1_ready, nth(4, a - 1, 2 * c + 1))
                pool.tensor_tensor(xb[:, QT * c:QT * c + QT], x_in[:, QT * c:QT * c + QT],
                                   b0_all[:, None, :].to_broadcast([P, QT, C]),
                                   ALU.add).then_inc(xb_ready, 1)

            def rstd_x(a, c):
                pool.wait_ge(st0_ready, nth(NC, a, c))
                pool.wait_ge(hf_ready, nth(KT, a - 1, QT * c + QT - 1))
                pool.tensor_tensor(rstd0[:, c], ve0[:, c], mhalf[:, 0:QT], ALU.pow).then_inc(pow0, 1)
                pool.wait_ge(pow0, nth(NC, a, c))
                pool.tensor_tensor(nmr0[:, c], nm0[:, c], rstd0[:, c], ALU.mult).then_inc(ln0_ready, 1)

            def setup():
                pool.memset(ident[:, :], 0.0).then_inc(ident_zero, 1)
                pool.memset(mhalf[:, :], -0.5)
                pool.wait_ge(ident_zero, 1)
                pool.affine_select(out=ident[:, :], in_=ident[:, :], compare_op=ALU.not_equal,
                                   fill=1.0, base=0, pattern=[[-1, P]],
                                   channel_multiplier=1).then_inc(ident_ready, 1)
                pool.wait_ge(ident_ready, 1)
                rstd_x(0, 0)
                rstd_x(0, 1)
                pool.wait_ge(biases_in, 4 * 16)
                add_b0(0, 0)

            def step(i, s, layer1, layer0, after, before):
                a = i + 1
                ready = relu_steps(i, s - 1, layer1, layer0)
                if ready:
                    n, c, pair = ready
                    r = QT * c + 2 * pair
                    pool.wait_ge(h1_ready, nth(KT, n, r + 1))
                    pool.tensor_tensor(x1[:, r:r + 2], x1[:, r:r + 2],
                                       bv_all[:, None, :].to_broadcast([P, 2, C]),
                                       ALU.add).then_inc(x1b_ready, 1)
                if s == 3 and layer0:
                    add_b0(a, 1)
                if s == 11 and after:
                    add_b0(a + 1, 0)
                if s == 6 and after:
                    rstd_x(a + 1, 0)
                if s == 13 and after:
                    rstd_x(a + 1, 1)
                norm = norm_steps(i, s, layer1, layer0)
                if norm:
                    n, c, pair = norm
                    pool.wait_ge(st1_ready, nth(4, n, 2 * c + pair))
                    pool.tensor_tensor(rstd1[:, pair], ve1[:, pair], mhalf[:, 0:2],
                                       ALU.pow).then_inc(pow1, 1)
                    pool.wait_ge(pow1, nth(4, n, 2 * c + pair))
                    pool.tensor_tensor(nmr1[:, pair], nm1[:, pair], rstd1[:, pair],
                                       ALU.mult).then_inc(ln1_ready, 1)

            turns(pool, step, setup)

        @block.scalar
        def _(act):
            def h0_relu(a, r):
                act.wait_ge(ln0_ready, nth(NC, a, r // QT))
                act.wait_ge(h0_ready, nth(KT, a, r - 2))
                act.activation(hf[:, r % 2], x_in[:, r], ACT.Relu,
                               bias=nmr0[:, r // QT, r % QT:r % QT + 1],
                               scale=rstd0[:, r // QT, r % QT:r % QT + 1]).then_inc(hf_ready, 1)

            def setup():
                for dst, src in ((w_f, w0), (wq_f, wq), (wk_f, wk), (wv_f, wv)):
                    act.dma_start(dst, src.rearrange("(t p) d -> p t d", p=P)).then_inc(weights_in, 16)
                act.dma_start(b0_all[:, :], b0.rearrange("(a d) -> a d", a=1)
                              .to_broadcast([P, C])).then_inc(biases_in, 16)
                act.dma_start(bv_all[:, :], bv.rearrange("(a d) -> a d", a=1)
                              .to_broadcast([P, C])).then_inc(biases_in, 16)
                with nc.allow_non_contiguous_dma(reason="two vectors of 256 down the partitions"):
                    act.dma_start(bqk[:, 0], bq.rearrange("(t p) -> p t", p=P)).then_inc(biases_in, 16)
                    act.dma_start(bqk[:, 1], bk.rearrange("(t p) -> p t", p=P)).then_inc(biases_in, 16)
                for r in range(6):
                    h0_relu(0, r)

            def step(i, s, layer1, layer0, after, before):
                b, a = i, i + 1
                c, t = s // KT, s % KT
                prep = prep_steps(i, s, layer1, layer0)
                if prep:
                    n, half = prep
                    cols = slice(Q * half, Q * half + Q)
                    for k, bank in enumerate((bank_t, bank_s)):
                        act.wait_ge(ht_done, nth(4, n, 2 * half + k))
                        act.activation(ht_hi[:, k, cols], bank[:, :], ACT.Copy).then_inc(ht_hi_ready, 1)
                    for k, bank in enumerate((bank_s, bank_t)):
                        act.wait_ge(z_done, nth(4, n, 2 * half + k))
                        act.activation(z_hi[:, k, cols], bank[:, :], ACT.Identity,
                                       bias=bz[:, k:k + 1]).then_inc(z_hi_ready, 1)
                    for k, bank in enumerate((bank_s, bank_t) * 2):
                        act.wait_ge(v_done, nth(KT, n, QT * half + k))
                        act.activation(v_hi[:, QT * half + k, 0:C], bank[:, 0:C],
                                       ACT.Copy).then_inc(v_hi_ready, 1)
                if layer1:
                    act.wait_ge(s_done, nth(TILES, b, s))
                    if t in (0, 4) and c == 0:
                        act.wait_ge(gk_ready, nth(KT, b, t + QT - 1))
                    act.activation(bank_s[:, :], bank_s[:, :], ACT.Exp,
                                   bias=gk[:, t:t + 1]).then_inc(exp_ready, 1)
                if t == 0 and (layer0 if c else layer1):
                    n = a if c else b
                    for k in range(CH):
                        if k == 0:
                            act.wait_ge(ah_done, nth(TILES, n, (s - 1) % TILES))
                        act.activation(g_hi[:, k], agg[:, k], ACT.Copy).then_inc(g_hi_ready, 1)
                if layer0:
                    act.wait_ge(tr_done, nth(TILES, a, s))
                    act.activation(a_hi[:, s % 2], bank_t[:, :], ACT.Copy).then_inc(a_hi_ready, 1)
                    if t % QT == 0:
                        act.wait_ge(rows_in[t // QT], nth(NC, a, c, 16))
                    act.wait_ge(rsum2_ready, nth(NC, a, c - 2 if t else c - 1))
                    act.activation(scrap[:, :], rows[:, t // QT, t % QT], ACT.Copy,
                                   accum_out=rsum[:, t // QT, t % QT:t % QT + 1]).then_inc(rsum_ready, 1)
                relu = relu_steps(i, s, layer1, layer0)
                if relu:
                    n, cc, pair = relu
                    act.wait_ge(ln1_ready, nth(4, n, 2 * cc + pair))
                    if pair == 0:
                        act.wait_ge(ht_done, nth(4, n, 2 * cc - 1))
                    for k in range(2):
                        r = 2 * pair + k
                        act.activation(h1[:, r], x1[:, QT * cc + r], ACT.Relu,
                                       bias=nmr1[:, pair, k:k + 1],
                                       scale=rstd1[:, pair, k:k + 1]).then_inc(h1_ready, 1)
                if layer0:
                    act.wait_ge(a_lo_ready, nth(TILES, a, s))
                    act.wait_ge(p_ready, nth(TILES, a - 1, s))
                    act.activation(a_t[:, c, t], bank_t[:, :], ACT.Copy).then_inc(a_t_ready, 1)
                h0 = h0_steps(i, s, layer0, after)
                if h0:
                    h0_relu(*h0)

            turns(act, step, setup)

        @block.vector
        def _(dve):
            def h0_split(a, r):
                dve.wait_ge(hf_ready, nth(KT, a, r))
                dve.wait_ge(ah_done, nth(TILES, a - 1, KT + r))
                dve.tensor_copy(h0_hi[:, r], hf[:, r % 2]).then_inc(h0_hi_ready, 1)
                dve.wait_ge(h0_hi_ready, nth(KT, a, r))
                dve.tensor_tensor(h0_lo[:, r], hf[:, r % 2], h0_hi[:, r],
                                  ALU.subtract).then_inc(h0_ready, 1)

            def stats_x(a, c):
                dve.wait_ge(x_got, nth(1, a, 0, 16))
                for r in range(QT):
                    dve.bn_stats(st0[:, r], x_in[:, QT * c + r]).then_inc(bn0, 1)
                dve.wait_ge(bn0, nth(KT, a, QT * c + QT - 1))

            def moments_x(a, c):
                for r in range(QT):
                    dve.bn_aggr(mv0[:, c, r], st0[:, r]).then_inc(mv0_ready, 1)
                dve.wait_ge(ln0_ready, nth(NC, a - 1, c))
                dve.wait_ge(mv0_ready, nth(KT, a, QT * c + QT - 1))
                dve.tensor_scalar(ve0[:, c], mv0[:, c, :, 1], EPS, None, ALU.add)
                dve.tensor_scalar(nm0[:, c], mv0[:, c, :, 0], -1.0, None, ALU.mult).then_inc(st0_ready, 1)

            links = [0]

            def link(ins):
                links[0] += 1
                ins.then_inc(setup_dve, 1)
                dve.wait_ge(setup_dve, links[0])

            def setup():
                dve.sem_inc(out_ready, 1)
                for c in range(NC):
                    stats_x(0, c)
                    moments_x(0, c)
                for r in range(6):
                    h0_split(0, r)
                dve.memset(ones[:, :], 1.0)
                dve.memset(v_hi[:, :, C:VW].bitcast(F32), 1.0)
                dve.memset(wv_hi[:, :, C + 1:VW].bitcast(F32), 0.0)
                dve.memset(wv_lo[:, :, C + 1:VW].bitcast(F32), 0.0)
                dve.wait_ge(biases_in, 4 * 16)
                dve.wait_ge(weights_in, 4 * 16)
                dve.tensor_tensor(bprod[:, :], bqk[:, 0], bqk[:, 1], ALU.mult).then_inc(bprod_ready, 1)
                link(dve.tensor_copy(w_hi[:, :, :], w_f))
                dve.tensor_tensor(w_lo[:, :, :], w_f, w_hi[:, :, :], ALU.subtract)
                dve.wait_ge(setup_pe, 1)
                for k in range(CH):
                    link(dve.tensor_copy(m_hi[:, k], att[:, k, 0:C]))
                    dve.tensor_tensor(m_lo[:, k], att[:, k, 0:C], m_hi[:, k], ALU.subtract)
                    link(dve.tensor_copy(wv_hi[:, k, 0:C + 1], att[:, CH + k, 0:C + 1]))
                    dve.tensor_tensor(wv_lo[:, k, 0:C + 1], att[:, CH + k, 0:C + 1],
                                      wv_hi[:, k, 0:C + 1], ALU.subtract)
                link(dve.tensor_copy(bz[:, :], att[:, 0, C:C + CH]))
                dve.tensor_copy(s0[:, :], att[:, 0, C + CH:C + CH + 1]).then_inc(weights_ready, 1)
                dve.wait_ge(weights_ready, 1)

            def step(i, s, layer1, layer0, after, before):
                b, a = i, i + 1
                c, t = s // KT, s % KT
                prep = prep_steps(i, s, layer1, layer0)
                if prep:
                    n, half = prep
                    cols = slice(Q * half, Q * half + Q)
                    for k, bank in enumerate((bank_t, bank_s)):
                        dve.wait_ge(ht_hi_ready, nth(4, n, 2 * half + k))
                        dve.tensor_tensor(ht_lo[:, k, cols], bank[:, :], ht_hi[:, k, cols],
                                          ALU.subtract).then_inc(ht_lo_ready, 1)
                    for k, bank in enumerate((bank_s, bank_t)):
                        dve.wait_ge(z_hi_ready, nth(4, n, 2 * half + k))
                        dve.scalar_tensor_tensor(z_lo[:, k, cols], bank[:, :], bz[:, k:k + 1],
                                                 z_hi[:, k, cols], ALU.add,
                                                 ALU.subtract).then_inc(z_lo_ready, 1)
                    for k, bank in enumerate((bank_s, bank_t) * 2):
                        kt = QT * half + k
                        dve.wait_ge(v_hi_ready, nth(KT, n, kt))
                        dve.tensor_tensor(v_lo[:, kt], bank[:, 0:C], v_hi[:, kt, 0:C],
                                          ALU.subtract).then_inc(v_lo_ready, 1)
                        dve.tensor_scalar(gk[:, kt:kt + 1], bank[:, C:C + 1], s0[:, 0:1], None,
                                          ALU.add).then_inc(gk_ready, 1)
                if layer1:
                    dve.wait_ge(exp_ready, nth(TILES, b, s))
                    dve.wait_ge(a_t_ready, nth(TILES, b, s))
                    dve.wait_ge(p_lo_ready, nth(TILES, b, s - 1))
                    dve.tensor_tensor(pf[:, :], bank_s[:, :], a_t[:, c, t], ALU.mult).then_inc(p_ready, 1)
                    dve.wait_ge(p_ready, nth(TILES, b, s))
                    dve.tensor_copy(p_hi[:, s % 2], pf[:, :]).then_inc(p_hi_ready, 1)
                norm = norm_steps(i, s, layer1, layer0)
                if norm:
                    n, cc, pair = norm
                    dve.wait_ge(y_done, nth(4, n, 2 * cc + pair))
                    dve.wait_ge(rinv0_ready, nth(NC, n, cc))
                    dve.wait_ge(xb_ready, nth(NC, n, cc))
                    for k in range(2):
                        r = 2 * pair + k
                        ins = dve.scalar_tensor_tensor(x1[:, QT * cc + r], bank_t[:, C * k:C * k + C],
                                                       rinv0[:, r:r + 1], xb[:, QT * cc + r],
                                                       ALU.mult, ALU.add)
                    ins.then_inc(x1_ready, 1)
                    dve.wait_ge(x1_ready, nth(4, n, 2 * cc + pair))
                    for k in range(2):
                        dve.bn_stats(st1[:, k], x1[:, QT * cc + 2 * pair + k]).then_inc(bn1, 1)
                    dve.wait_ge(bn1, nth(KT, n, QT * cc + 2 * pair + 1))
                if s in (6, 13) and after:
                    stats_x(a + 1, s // KT)
                if layer1:
                    dve.wait_ge(p_hi_ready, nth(TILES, b, s))
                    dve.tensor_tensor(p_lo[:, s % 2], pf[:, :], p_hi[:, s % 2],
                                      ALU.subtract).then_inc(p_lo_ready, 1)
                if t == 0 and (layer0 if c else layer1):
                    n = a if c else b
                    for k in range(CH):
                        dve.wait_ge(g_hi_ready, nth(4, n, 2 * (1 - c) + k))
                        dve.tensor_tensor(g_lo[:, k], agg[:, k], g_hi[:, k],
                                          ALU.subtract).then_inc(g_lo_ready, 1)
                    dve.wait_ge(rsum_ready, nth(TILES, n, (s - 1) % TILES))
                    dve.tensor_tensor(rsum2[:, :], rsum[:, 0], rsum[:, 1], ALU.add).then_inc(rsum2_ready, 1)
                    dve.wait_ge(rsum2_ready, nth(NC, n, 1 - c))
                    dve.reciprocal(rinv0[:, :], rsum2[:, :]).then_inc(rinv0_ready, 1)
                if layer0:
                    dve.wait_ge(a_hi_ready, nth(TILES, a, s))
                    dve.tensor_tensor(a_lo[:, s % 2], bank_t[:, :], a_hi[:, s % 2],
                                      ALU.subtract).then_inc(a_lo_ready, 1)
                if norm:
                    n, cc, pair = norm
                    for k in range(2):
                        dve.bn_aggr(mv1[:, pair, k], st1[:, k]).then_inc(mv1_ready, 1)
                    dve.wait_ge(mv1_ready, nth(KT, n, QT * cc + 2 * pair + 1))
                    dve.tensor_scalar(ve1[:, pair], mv1[:, pair, :, 1], EPS, None, ALU.add)
                    dve.tensor_scalar(nm1[:, pair], mv1[:, pair, :, 0], -1.0, None,
                                      ALU.mult).then_inc(st1_ready, 1)
                if s in (6, 13) and after:
                    moments_x(a + 1, s // KT)
                h0 = h0_steps(i, s, layer0, after)
                if h0:
                    h0_split(*h0)
                if t == 0 and (before if c == 0 else layer1):
                    ob = b - 1 if c == 0 else b
                    oc = 1 - c
                    dve.wait_ge(pv_done, nth(TILES, ob, (s - 1) % TILES))
                    dve.reciprocal(rinv1[:, :], att[:, :, C]).then_inc(rinv1_ready, 1)
                    dve.wait_ge(rinv1_ready, nth(NC, ob, oc))
                    dve.wait_ge(x1b_ready, nth(4, ob, 2 * oc + 1))
                    dve.wait_ge(stored, nth(NC, ob, oc, 16))
                    for r in range(QT):
                        ins = dve.scalar_tensor_tensor(o_sb[:, r], att[:, r, 0:C], rinv1[:, r:r + 1],
                                                       x1[:, QT * oc + r], ALU.mult, ALU.add)
                    ins.then_inc(out_ready, 1)

            turns(dve, step, setup)

        @block.tensor
        def _(pe):
            def three(dst, l_hi, l_lo, r_hi, r_lo, start, stop):
                n = r_lo.shape[-1]
                pe.matmul(dst, l_hi, r_hi, start=start, stop=False)
                pe.matmul(dst[:, 0:n], l_hi, r_lo, start=False, stop=False)
                return pe.matmul(dst, l_lo, r_hi, start=False, stop=stop)

            def setup():
                pe.wait_ge(ident_ready, 1)
                pe.wait_ge(bprod_ready, 1)
                pe.wait_ge(biases_in, 4 * 16)
                pe.wait_ge(weights_in, 4 * 16)
                for k in range(CH):
                    ch = slice(P * k, P * k + P)
                    for o in range(CH):
                        pe.matmul(att[:, k, 0:C], wk_f[:, o, ch], wq_f[:, o, :],
                                  start=(o == 0), stop=(o == CH - 1))
                    for o in range(CH):
                        pe.transpose(att[:, CH + k, P * o:P * o + P], wv_f[:, o, ch], ident[:, :])
                    for o in range(CH):
                        pe.matmul(att[:, CH + k, C:C + 1], wk_f[:, o, ch], bqk[:, 0, o:o + 1],
                                  start=(o == 0), stop=(o == CH - 1))
                for k in range(CH):
                    for o in range(CH):
                        pe.matmul(att[:, 0, C + k:C + k + 1], wq_f[:, o, P * k:P * k + P],
                                  bqk[:, 1, o:o + 1], start=(o == 0), stop=(o == CH - 1))
                for o in range(CH):
                    mm = pe.matmul(att[:, 0, C + CH:C + CH + 1], ones[:, :], bprod[:, o:o + 1],
                                   start=(o == 0), stop=(o == CH - 1))
                mm.then_inc(setup_pe, 1)
                pe.wait_ge(weights_ready, 1)

            def step(i, s, layer1, layer0, after, before):
                b, a = i, i + 1
                c, t = s // KT, s % KT

                def free_t_of_transposes(n, tile):
                    pe.wait_ge(a_t_ready, nth(TILES, n, tile))

                def scores():
                    if prep:
                        pe.wait_ge(gk_ready, nth(KT, prep[0], QT * prep[1] + 2))
                    elif s == 0:
                        pe.wait_ge(p_ready, nth(TILES, b - 1, TILES - 1))
                    else:
                        pe.wait_ge(p_ready, nth(TILES, b, s - 1))
                    for k in range(CH):
                        mm = three(bank_s[:, :], z_hi[:, k, P * t:P * t + P], z_lo[:, k, P * t:P * t + P],
                                   ht_hi[:, k, Q * c:Q * c + Q], ht_lo[:, k, Q * c:Q * c + Q],
                                   k == 0, k == CH - 1)
                    mm.then_inc(s_done, 1)

                def aggregate(n, tile):
                    m = tile % KT
                    if m == 0:
                        pe.wait_ge(g_lo_ready, nth(4, n, 4 * (tile // KT) // 2 - 1))
                    if tile < KT:
                        pe.wait_ge(h0_ready, nth(KT, n, m))
                    pe.wait_ge(a_lo_ready, nth(TILES, n, tile))
                    for k in range(CH):
                        ch = slice(P * k, P * k + P)
                        mm = three(agg[:, k], h0_hi[:, m, ch], h0_lo[:, m, ch],
                                   a_hi[:, tile % 2], a_lo[:, tile % 2], m == 0, m == KT - 1)
                    mm.then_inc(ah_done, 1)

                def transposes():
                    if t % QT == 0:
                        pe.wait_ge(rows_in[t // QT], nth(NC, a, c, 16))
                    if norm:
                        pe.wait_ge(x1_ready, nth(4, norm[0], 2 * norm[1] + norm[2]))
                    elif prep:
                        pe.wait_ge(gk_ready, nth(KT, prep[0], QT * prep[1] + 3))
                    else:
                        free_t_of_transposes(a, s - 1)
                    h, m = t // QT, t % QT
                    for r in range(QT):
                        mm = pe.transpose(bank_t[:, P * r:P * r + P], rows[:, h, r, P * m:P * m + P],
                                          ident[:, :])
                    mm.then_inc(tr_done, 1)

                def values(n, tile):
                    kt = tile % KT
                    if kt == 0:
                        pe.wait_ge(out_ready, nth(NC, n, tile // KT))
                    pe.wait_ge(p_lo_ready, nth(TILES, n, tile))
                    for r in range(QT):
                        q = slice(P * r, P * r + P)
                        mm = three(att[:, r, 0:VW], p_hi[:, tile % 2, q], p_lo[:, tile % 2, q],
                                   v_hi[:, kt], v_lo[:, kt], kt == 0, kt == KT - 1)
                    mm.then_inc(pv_done, 1)

                def y_pair(n, cc, pair):
                    pe.wait_ge(g_lo_ready, nth(4, n, 2 * cc + 1))
                    if layer0:
                        free_t_of_transposes(a, s - 1)
                    elif pair:
                        pe.wait_ge(x1_ready, nth(4, n, 2 * cc))
                    else:
                        free_t_of_transposes(n, TILES - 1)
                    for r in range(2):
                        q = slice(P * (2 * pair + r), P * (2 * pair + r) + P)
                        for k in range(CH):
                            mm = three(bank_t[:, C * r:C * r + C], g_hi[:, k, q], g_lo[:, k, q],
                                       w_hi[:, k], w_lo[:, k], k == 0, k == CH - 1)
                    mm.then_inc(y_done, 1)

                def prep_transposes(n, half):
                    pe.wait_ge(h1_ready, nth(KT, n, QT * half + QT - 1))
                    if layer0:
                        free_t_of_transposes(a, s - 1)
                    for k, bank in enumerate((bank_t, bank_s)):
                        if k and layer1:
                            pe.wait_ge(p_ready, nth(TILES, b, s - 1))
                        for r in range(QT):
                            mm = pe.transpose(bank[:, P * r:P * r + P], h1[:, r, P * k:P * k + P],
                                              ident[:, :])
                        mm.then_inc(ht_done, 1)

                def prep_z_and_v(n, half):
                    cols = slice(Q * half, Q * half + Q)
                    pe.wait_ge(ht_lo_ready, nth(4, n, 2 * half + 1))
                    for d, bank in enumerate((bank_s, bank_t)):
                        for k in range(CH):
                            dd = slice(P * d, P * d + P)
                            mm = three(bank[:, :], m_hi[:, k, dd], m_lo[:, k, dd],
                                       ht_hi[:, k, cols], ht_lo[:, k, cols], k == 0, k == CH - 1)
                        mm.then_inc(z_done, 1)
                    for r, bank in enumerate((bank_s, bank_t) * 2):
                        if r < 2:
                            pe.wait_ge(z_lo_ready, nth(4, n, 2 * half + r))
                        else:
                            pe.wait_ge(gk_ready, nth(KT, n, QT * half + r - 2))
                        kt = QT * half + r
                        for k in range(CH):
                            mm = three(bank[:, 0:VW], ht_hi[:, k, P * kt:P * kt + P],
                                       ht_lo[:, k, P * kt:P * kt + P], wv_hi[:, k], wv_lo[:, k],
                                       k == 0, k == CH - 1)
                        mm.then_inc(v_done, 1)

                norm = norm_steps(i, s, layer1, layer0)
                prep = prep_steps(i, s, layer1, layer0)
                late = (b - 1, TILES - 1) if s == 0 else (b, s - 1)
                has_late = before if s == 0 else layer1
                agg_of = (b, TILES - 1) if s == 0 else (a, s - 1)
                has_agg = layer1 if s == 0 else layer0
                if prep:
                    prep_transposes(*prep)
                    if has_late:
                        values(*late)
                    prep_z_and_v(*prep)
                if layer1:
                    scores()
                if norm:
                    y_pair(*norm)
                if has_agg:
                    aggregate(*agg_of)
                if layer0:
                    transposes()
                if has_late and not prep:
                    values(*late)

            turns(pe, step, setup)


_INS = ["x", "adj", "L0_gnn_W", "L0_gnn_b", "L1_gnn_Wq_w", "L1_gnn_Wq_b", "L1_gnn_Wk_w",
        "L1_gnn_Wk_b", "L1_gnn_Wv_w", "L1_gnn_Wv_b"]


def kernel(**inputs):
    import numpy as _np
    import concourse.bacc as _bacc
    from concourse.bass_utils import run_bass_kernel_spmd as _run

    nc = _bacc.Bacc("TRN2", target_bir_lowering=False, num_devices=1)
    arrays, args = {}, []
    for name in _INS:
        a = _np.ascontiguousarray(inputs[name])
        arrays[f"in_{name}_dram"] = a
        args.append(nc.dram_tensor(f"in_{name}_dram", a.shape, mybir.dt.from_np(a.dtype),
                                   kind="ExternalInput").ap())
    out = nc.dram_tensor("out_dram", inputs["x"].shape, F32, kind="ExternalOutput").ap()
    build(nc, *args, out)
    r = _run(nc, [arrays], core_ids=[0])
    return r.results[0]["out_dram"]
```

```python
import concourse.bass as bass
from concourse import mybir
from contextlib import ExitStack

F32 = mybir.dt.float32
F32R = mybir.dt.float32r
ALU = mybir.AluOpType
ACT = mybir.ActivationFunctionType
AX = mybir.AxisListType

P = 128
EPS = 1e-5


def build(nc, x, adj, w0, b0, wq, bq, wk, bk, wv, bv, out):
    B, N, C = x.shape
    CH = C // P
    Q = 512
    NC = N // Q
    KT = N // P
    QT = Q // P
    TILES = NC * KT
    MH = N // Q
    VW = C + 2
    assert (CH, NC, KT, QT, TILES, MH) == (2, 2, 8, 4, 16, 2)
    LOOPS = B - 2

    adj_v = adj.rearrange("b (c r p) (h m) -> b c h p r m", c=NC, p=P, h=MH)
    x_v = x.rearrange("b (r p) d -> b p r d", p=P)
    out_v = out.rearrange("b (c r p) d -> b c p r d", c=NC, p=P)

    with ExitStack() as ctx:
        def sb(name, shape, dt=F32):
            return ctx.enter_context(nc.sbuf_tensor(name, shape, dt))

        def ps(name, shape):
            return ctx.enter_context(nc.psum_tensor(name, shape, F32))

        def sem(name):
            return ctx.enter_context(nc.semaphore(name))

        rows = sb("rows", [P, MH, QT, Q])
        a_t = sb("a_t", [P, NC, KT, Q])
        a_hi = sb("a_hi", [P, 2, Q], F32R)
        a_lo = sb("a_lo", [P, 2, Q], F32R)
        x_in = sb("x_in", [P, KT, C])
        xb = sb("xb", [P, KT, C])
        hf = sb("hf", [P, 2, C])
        h0_hi = sb("h0_hi", [P, KT, C], F32R)
        h0_lo = sb("h0_lo", [P, KT, C], F32R)
        g_hi = sb("g_hi", [P, CH, Q], F32R)
        g_lo = sb("g_lo", [P, CH, Q], F32R)
        scrap = sb("scrap", [P, Q])
        rsum = sb("rsum", [P, NC, MH, QT])
        rsum2 = sb("rsum2", [P, QT])
        rinv0 = sb("rinv0", [P, QT])
        x1 = sb("x1", [P, KT, C])
        h1 = sb("h1", [P, QT, C])
        ht_hi = sb("ht_hi", [P, CH, N], F32R)
        ht_lo = sb("ht_lo", [P, CH, N], F32R)
        z_hi = sb("z_hi", [P, CH, N], F32R)
        z_lo = sb("z_lo", [P, CH, N], F32R)
        v_hi = sb("v_hi", [P, KT, VW], F32R)
        v_lo = sb("v_lo", [P, KT, C], F32R)
        gk = sb("gk", [P, KT])
        pf = sb("pf", [P, Q])
        p_hi = sb("p_hi", [P, 2, Q], F32R)
        p_lo = sb("p_lo", [P, 2, Q], F32R)
        rinv1 = sb("rinv1", [P, QT])
        o_sb = sb("o_sb", [P, QT, C])
        st0 = sb("st0", [P, QT, 6])
        mv0 = sb("mv0", [P, NC, QT, 2])
        ve0 = sb("ve0", [P, NC, QT])
        nm0 = sb("nm0", [P, NC, QT])
        rstd0 = sb("rstd0", [P, NC, QT])
        nmr0 = sb("nmr0", [P, NC, QT])
        st1 = sb("st1", [P, 2, 6])
        mv1 = sb("mv1", [P, 2, 2, 2])
        ve1 = sb("ve1", [P, 2, 2])
        nm1 = sb("nm1", [P, 2, 2])
        rstd1 = sb("rstd1", [P, 2, 2])
        nmr1 = sb("nmr1", [P, 2, 2])
        ident = sb("ident", [P, P])
        ones = sb("ones", [P, P])
        mhalf = sb("mhalf", [P, QT])
        w_hi = sb("w_hi", [P, CH, C], F32R)
        w_lo = sb("w_lo", [P, CH, C], F32R)
        m_hi = sb("m_hi", [P, CH, C], F32R)
        m_lo = sb("m_lo", [P, CH, C], F32R)
        wv_hi = sb("wv_hi", [P, CH, VW], F32R)
        wv_lo = sb("wv_lo", [P, CH, VW], F32R)
        b0_all = sb("b0_all", [P, C])
        bv_all = sb("bv_all", [P, C])
        bqk = sb("bqk", [P, 2, CH])
        bprod = sb("bprod", [P, CH])
        bz = sb("bz", [P, CH])
        s0 = sb("s0", [P, 1])
        w_f = x1[:, 0:CH, :]
        wq_f = x1[:, CH:2 * CH, :]
        wk_f = x1[:, 2 * CH:3 * CH, :]
        wv_f = x1[:, 3 * CH:4 * CH, :]

        bank_t = ps("bank_t", [P, Q])
        bank_s = ps("bank_s", [P, Q])
        agg = ps("agg", [P, CH, Q])
        att = ps("att", [P, QT, Q])

        rows_in = [sem(f"rows_in{h}") for h in range(MH)]
        x_got = sem("x_got")
        weights_in = sem("weights_in")
        biases_in = sem("biases_in")
        stored = sem("stored")
        ident_zero = sem("ident_zero")
        ident_ready = sem("ident_ready")
        bprod_ready = sem("bprod_ready")
        setup_pe = sem("setup_pe")
        setup_dve = sem("setup_dve")
        weights_ready = sem("weights_ready")
        tr_done = sem("tr_done")
        ah_done = sem("ah_done")
        y_done = sem("y_done")
        ht_done = sem("ht_done")
        z_done = sem("z_done")
        v_done = sem("v_done")
        s_done = sem("s_done")
        pv_done = sem("pv_done")
        a_hi_ready = sem("a_hi_ready")
        a_t_ready = sem("a_t_ready")
        rsum_ready = sem("rsum_ready")
        exp_ready = sem("exp_ready")
        g_hi_ready = sem("g_hi_ready")
        ht_hi_ready = sem("ht_hi_ready")
        z_hi_ready = sem("z_hi_ready")
        v_hi_ready = sem("v_hi_ready")
        hf_ready = sem("hf_ready")
        h1_ready = sem("h1_ready")
        half_att_read = sem("half_att_read")
        a_lo_ready = sem("a_lo_ready")
        p_ready = sem("p_ready")
        p_hi_ready = sem("p_hi_ready")
        p_lo_ready = sem("p_lo_ready")
        g_lo_ready = sem("g_lo_ready")
        rsum2_ready = sem("rsum2_ready")
        rinv0_ready = sem("rinv0_ready")
        ht_lo_ready = sem("ht_lo_ready")
        z_lo_ready = sem("z_lo_ready")
        v_lo_ready = sem("v_lo_ready")
        gk_ready = sem("gk_ready")
        h0_hi_ready = sem("h0_hi_ready")
        h0_ready = sem("h0_ready")
        x1_ready = sem("x1_ready")
        x1_tile = sem("x1_tile")
        bn0 = sem("bn0")
        mv0_ready = sem("mv0_ready")
        st0_ready = sem("st0_ready")
        bn1 = sem("bn1")
        mv1_ready = sem("mv1_ready")
        st1_ready = sem("st1_ready")
        rinv1_ready = sem("rinv1_ready")
        half_out_ready = sem("half_out_ready")
        out_ready = sem("out_ready")
        pow0 = sem("pow0")
        ln0_ready = sem("ln0_ready")
        pow1 = sem("pow1")
        ln1_ready = sem("ln1_ready")
        xb_ready = sem("xb_ready")
        x1b_ready = sem("x1b_ready")

        def nth(per, batch, n, by=1):
            value = (batch * per + (n + 1)) * by
            return max(value, 0) if isinstance(value, int) else value

        def turns(eng, step, setup):
            setup()
            for s in range(TILES):
                step(-1, s, False, True, True, False)
            for s in range(2):
                step(0, s, True, True, True, False)
            with eng.Fori(0, LOOPS) as i:
                for s in range(2, TILES):
                    step(i, s, True, True, True, True)
                for s in range(2):
                    step(i + 1, s, True, True, True, True)
            for s in range(2, TILES):
                step(B - 2, s, True, True, False, True)
            for s in range(2):
                step(B - 1, s, True, False, False, True)
            for s in range(2, TILES):
                step(B - 1, s, True, False, False, True)
            for s in range(2):
                step(B, s, False, False, False, True)

        def norm_steps(i, s, layer1, layer0):
            if s in (1, 2) and layer1:
                return i, 1, s - 1
            if s in (9, 10) and layer0:
                return i + 1, 0, s - 9
            return None

        def relu_steps(i, s, layer1, layer0):
            return norm_steps(i, s - 1, layer1, layer0)

        def side_steps(i, s, layer1, layer0):
            if s == 12 and layer0:
                return "h", i + 1, 1
            if s == 13 and layer0:
                return "z", i + 1, 1
            if s in (0, 5) and layer1:
                return "v", i, 3 if s == 0 else 5
            return None

        def end_steps(i, s, layer1, layer0):
            if s in (11, 12) and layer0:
                return "hz"[s - 11], i + 1, 0
            if s in (13, 14, 15) and layer0:
                return "v", i + 1, s - 13
            if s in (5, 6) and layer1:
                return "v", i, s + 1
            return None

        def h0_steps(i, s, layer0, after):
            if s >= 12 and after:
                return [(i + 2, s - 12)]
            if s in (2, 4) and layer0:
                return [(i + 1, 3 + s // 2)]
            if s == 5 and layer0:
                return [(i + 1, 6), (i + 1, 7)]
            return []

        def score_bank(s, layer0):
            return agg[:, 0] if not layer0 and s >= 3 and s % 2 else bank_s[:, :]

        EVENTS = {"h": 4, "z": 4, "v": KT}

        block = ctx.enter_context(nc.Block())

        @block.sync
        def _(sp):
            def load_rows(a, c, h):
                sp.dma_start(rows[:, h], adj_v[a, c, h]).then_inc(rows_in[h], 16)

            def load_x(a):
                sp.dma_start(x_in[:, :, :], x_v[a]).then_inc(x_got, 16)

            def setup():
                sp.sem_inc(stored, 16)
                load_x(0)
                load_rows(0, 0, 0)
                sp.dma_start(b0_all[:, :], b0.rearrange("(a d) -> a d", a=1)
                             .to_broadcast([P, C])).then_inc(biases_in, 16)
                sp.dma_start(bv_all[:, :], bv.rearrange("(a d) -> a d", a=1)
                             .to_broadcast([P, C])).then_inc(biases_in, 16)
                with nc.allow_non_contiguous_dma(reason="two vectors of 256 down the partitions"):
                    sp.dma_start(bqk[:, 0], bq.rearrange("(t p) -> p t", p=P)).then_inc(biases_in, 16)
                    sp.dma_start(bqk[:, 1], bk.rearrange("(t p) -> p t", p=P)).then_inc(biases_in, 16)
                for dst, src in ((w_f, w0), (wq_f, wq), (wk_f, wk), (wv_f, wv)):
                    sp.dma_start(dst, src.rearrange("(t p) d -> p t d", p=P)).then_inc(weights_in, 16)
                load_rows(0, 0, 1)

            def step(i, s, layer1, layer0, after, before):
                b, a = i, i + 1
                c, t = s // KT, s % KT
                if s == 5 and after:
                    sp.wait_ge(xb_ready, nth(NC, a, 1))
                    sp.wait_ge(hf_ready, nth(KT, a, KT - 1))
                    load_x(a + 1)
                if t in (3, 7) and (layer0 if c == 0 else after):
                    sp.wait_ge(tr_done, nth(TILES, a, s))
                    sp.wait_ge(rsum_ready, nth(TILES, a, s))
                    load_rows(a + c, 1 - c, t // QT)
                if t == 1 and (before if c == 0 else layer1):
                    ob = b - 1 if c == 0 else b
                    sp.wait_ge(out_ready, nth(NC, ob, 2 - c))
                    sp.dma_start(out_v[ob, 1 - c], o_sb[:, :, :]).then_inc(stored, 16)

            turns(sp, step, setup)
            sp.wait_ge(stored, nth(NC, B - 1, NC, 16))

        @block.gpsimd
        def _(pool):
            def add_b0(a, c):
                pool.wait_ge(x_got, nth(1, a, 0, 16))
                pool.wait_ge(x1_ready, nth(4, a - 1, 2 * c + 1))
                pool.tensor_tensor(xb[:, QT * c:QT * c + QT], x_in[:, QT * c:QT * c + QT],
                                   b0_all[:, None, :].to_broadcast([P, QT, C]),
                                   ALU.add).then_inc(xb_ready, 1)

            def rstd_x(a, c):
                pool.wait_ge(st0_ready, nth(NC, a, c))
                pool.wait_ge(hf_ready, nth(KT, a - 1, QT * c + QT - 1))
                pool.tensor_tensor(rstd0[:, c], ve0[:, c], mhalf[:, 0:QT], ALU.pow).then_inc(pow0, 1)
                pool.wait_ge(pow0, nth(NC, a, c))
                pool.tensor_tensor(nmr0[:, c], nm0[:, c], rstd0[:, c], ALU.mult).then_inc(ln0_ready, 1)

            def setup():
                pool.memset(ident[:, :], 0.0).then_inc(ident_zero, 1)
                pool.memset(mhalf[:, :], -0.5)
                pool.wait_ge(ident_zero, 1)
                pool.affine_select(out=ident[:, :], in_=ident[:, :], compare_op=ALU.not_equal,
                                   fill=1.0, base=0, pattern=[[-1, P]],
                                   channel_multiplier=1).then_inc(ident_ready, 1)
                pool.wait_ge(ident_ready, 1)
                rstd_x(0, 0)
                rstd_x(0, 1)
                pool.wait_ge(biases_in, 4 * 16)
                add_b0(0, 0)

            def step(i, s, layer1, layer0, after, before):
                b, a = i, i + 1
                c, t = s // KT, s % KT
                if t == 1 and (before if c == 0 else layer1):
                    ob, oc = (b, 0) if c else (b - 1, 1)
                    pool.wait_ge(half_out_ready, nth(NC, ob, oc))
                    pool.wait_ge(half_att_read, nth(NC, ob, oc))
                    pool.wait_ge(x1b_ready, nth(4, ob, 2 * oc + 1))
                    pool.tensor_tensor(o_sb[:, 2:QT], o_sb[:, 2:QT], x1[:, QT * oc + 2:QT * oc + QT],
                                       ALU.add).then_inc(out_ready, 1)
                if s in (11, 14) and after:
                    rstd_x(a + 1, 0 if s == 11 else 1)
                ready = relu_steps(i, s - 1, layer1, layer0)
                if ready:
                    n, c, pair = ready
                    r = QT * c + 2 * pair
                    pool.wait_ge(h1_ready, nth(KT, n, r + 1))
                    pool.tensor_tensor(x1[:, r:r + 2], x1[:, r:r + 2],
                                       bv_all[:, None, :].to_broadcast([P, 2, C]),
                                       ALU.add).then_inc(x1b_ready, 1)
                if s == 3 and layer0:
                    add_b0(a, 1)
                if s == 11 and after:
                    add_b0(a + 1, 0)
                norm = norm_steps(i, s, layer1, layer0)
                if norm:
                    n, c, pair = norm
                    pool.wait_ge(st1_ready, nth(4, n, 2 * c + pair))
                    pool.tensor_tensor(rstd1[:, pair], ve1[:, pair], mhalf[:, 0:2],
                                       ALU.pow).then_inc(pow1, 1)
                    pool.wait_ge(pow1, nth(4, n, 2 * c + pair))
                    pool.tensor_tensor(nmr1[:, pair], nm1[:, pair], rstd1[:, pair],
                                       ALU.mult).then_inc(ln1_ready, 1)

            turns(pool, step, setup)

        @block.scalar
        def _(act):
            def h0_relu(a, r):
                act.wait_ge(ln0_ready, nth(NC, a, r // QT))
                act.wait_ge(h0_ready, nth(KT, a, r - 2))
                act.activation(hf[:, r % 2], x_in[:, r], ACT.Relu,
                               bias=nmr0[:, r // QT, r % QT:r % QT + 1],
                               scale=rstd0[:, r // QT, r % QT:r % QT + 1]).then_inc(hf_ready, 1)

            def row_sums(a, s):
                c, t = s // KT, s % KT
                if t % QT == 0:
                    act.wait_ge(rows_in[t // QT], nth(NC, a, c, 16))
                if t == 0:
                    act.wait_ge(rsum2_ready, nth(NC, a - 1, c))
                act.wait_ge(rsum_ready, nth(TILES, a, s - 1))
                act.activation(scrap[:, :], rows[:, t // QT, t % QT], ACT.Copy,
                               accum_out=rsum[:, c, t // QT, t % QT:t % QT + 1]).then_inc(rsum_ready, 1)

            def h1_relu(n, cc, pair):
                act.wait_ge(ln1_ready, nth(4, n, 2 * cc + pair))
                if pair == 0:
                    act.wait_ge(ht_done, nth(4, n, 2 * cc - 1))
                for k in range(2):
                    r = 2 * pair + k
                    act.activation(h1[:, r], x1[:, QT * cc + r], ACT.Relu,
                                   bias=nmr1[:, pair, k:k + 1],
                                   scale=rstd1[:, pair, k:k + 1]).then_inc(h1_ready, 1)

            def operation_hi(op, bank):
                kind, n, x = op
                cols = slice(Q * (x // 2), Q * (x // 2) + Q)
                if kind == "h":
                    act.wait_ge(ht_done, nth(4, n, x))
                    act.activation(ht_hi[:, x % 2, cols], bank[:, :], ACT.Copy).then_inc(ht_hi_ready, 1)
                elif kind == "z":
                    act.wait_ge(z_done, nth(4, n, x))
                    act.activation(z_hi[:, x % 2, cols], bank[:, :], ACT.Identity,
                                   bias=bz[:, x % 2:x % 2 + 1]).then_inc(z_hi_ready, 1)
                else:
                    act.wait_ge(v_done, nth(KT, n, x))
                    act.activation(v_hi[:, x, 0:C], bank[:, 0:C], ACT.Copy).then_inc(v_hi_ready, 1)

            def setup():
                for r in range(QT):
                    h0_relu(0, r)

            def step(i, s, layer1, layer0, after, before):
                b, a = i, i + 1
                c, t = s // KT, s % KT
                side = side_steps(i, s, layer1, layer0)
                end = end_steps(i, s, layer1, layer0)
                spare = bank_t if layer1 or not layer0 else bank_s
                if s == 4 and layer1:
                    operation_hi(("h", b, 2), bank_t)
                    operation_hi(("h", b, 3), bank_s)
                    if layer0:
                        row_sums(a, s - 1)
                    operation_hi(("z", b, 2), bank_t)
                    operation_hi(("z", b, 3), bank_s)
                    operation_hi(("v", b, 4), bank_t)
                if side and s == 5:
                    operation_hi(side, spare)
                if layer1:
                    act.wait_ge(s_done, nth(TILES, b, s))
                    if c == 0:
                        act.wait_ge(gk_ready, nth(KT, b, t))
                    act.activation(score_bank(s, layer0), score_bank(s, layer0), ACT.Exp,
                                   bias=gk[:, t:t + 1]).then_inc(exp_ready, 1)
                if side and s != 5:
                    operation_hi(side, spare)
                relu = relu_steps(i, s, layer1, layer0)
                if relu:
                    h1_relu(*relu)
                if s == 0 and layer1:
                    row_sums(b, TILES - 1)
                elif s > 0 and layer0 and not (s in (3, 4) and layer1):
                    row_sums(a, s - 1)
                h0s = h0_steps(i, s, layer0, after)
                if s >= KT:
                    for h0 in h0s:
                        h0_relu(*h0)
                if t == 0 and (layer0 if c else layer1):
                    n = a if c else b
                    for k in range(CH):
                        if k == 0:
                            act.wait_ge(ah_done, nth(TILES, n, (s - 1) % TILES))
                        act.activation(g_hi[:, k], agg[:, k], ACT.Copy).then_inc(g_hi_ready, 1)
                if layer0:
                    act.wait_ge(p_ready, nth(TILES, a - 1, s))
                    act.wait_ge(tr_done, nth(TILES, a, s))
                    act.activation(a_t[:, c, t], bank_t[:, :], ACT.Copy).then_inc(a_t_ready, 1)
                    act.wait_ge(a_t_ready, nth(TILES, a, s))
                    act.activation(a_hi[:, s % 2], a_t[:, c, t], ACT.Copy).then_inc(a_hi_ready, 1)
                if s == 3 and layer0 and layer1:
                    row_sums(a, s - 1)
                if t == 0 and (before if c == 0 else layer1):
                    ob, oc = (b, 0) if c else (b - 1, 1)
                    act.wait_ge(rinv1_ready, nth(NC, ob, oc))
                    act.wait_ge(stored, nth(NC, ob, oc, 16))
                    for r in range(2, QT):
                        ins = act.activation(o_sb[:, r], att[:, r, 0:C], ACT.Identity,
                                             scale=rinv1[:, r:r + 1])
                    ins.then_inc(half_att_read, 1)
                if s < KT:
                    for h0 in h0s:
                        h0_relu(*h0)
                if end:
                    operation_hi(end, spare)

            turns(act, step, setup)

        @block.vector
        def _(dve):
            def h0_split(a, r):
                dve.wait_ge(hf_ready, nth(KT, a, r))
                dve.wait_ge(ah_done, nth(TILES, a - 1, KT + r))
                dve.tensor_copy(h0_hi[:, r], hf[:, r % 2]).then_inc(h0_hi_ready, 1)
                dve.wait_ge(h0_hi_ready, nth(KT, a, r))
                dve.tensor_tensor(h0_lo[:, r], hf[:, r % 2], h0_hi[:, r],
                                  ALU.subtract).then_inc(h0_ready, 1)

            def stats_x(a, r0, tiles):
                dve.wait_ge(x_got, nth(1, a, 0, 16))
                for r in range(r0, r0 + tiles):
                    dve.bn_stats(st0[:, r % QT], x_in[:, r]).then_inc(bn0, 1)
                dve.wait_ge(bn0, nth(KT, a, r0 + tiles - 1))

            def moments_x(a, c):
                for r in range(QT):
                    dve.bn_aggr(mv0[:, c, r], st0[:, r]).then_inc(mv0_ready, 1)
                dve.wait_ge(ln0_ready, nth(NC, a - 1, c))
                dve.wait_ge(mv0_ready, nth(KT, a, QT * c + QT - 1))
                dve.tensor_scalar(ve0[:, c], mv0[:, c, :, 1], EPS, None, ALU.add)
                dve.tensor_scalar(nm0[:, c], mv0[:, c, :, 0], -1.0, None, ALU.mult).then_inc(st0_ready, 1)

            links = [0]

            def link(ins):
                links[0] += 1
                ins.then_inc(setup_dve, 1)
                dve.wait_ge(setup_dve, links[0])

            def operation_lo(op, bank):
                kind, n, x = op
                cols = slice(Q * (x // 2), Q * (x // 2) + Q)
                if kind == "h":
                    dve.wait_ge(ht_hi_ready, nth(4, n, x))
                    dve.tensor_tensor(ht_lo[:, x % 2, cols], bank[:, :], ht_hi[:, x % 2, cols],
                                      ALU.subtract).then_inc(ht_lo_ready, 1)
                elif kind == "z":
                    dve.wait_ge(z_hi_ready, nth(4, n, x))
                    dve.scalar_tensor_tensor(z_lo[:, x % 2, cols], bank[:, :], bz[:, x % 2:x % 2 + 1],
                                             z_hi[:, x % 2, cols], ALU.add,
                                             ALU.subtract).then_inc(z_lo_ready, 1)
                else:
                    dve.wait_ge(v_hi_ready, nth(KT, n, x))
                    dve.tensor_scalar(gk[:, x:x + 1], bank[:, C:C + 1], s0[:, 0:1], None,
                                      ALU.add).then_inc(gk_ready, 1)
                    dve.tensor_tensor(v_lo[:, x], bank[:, 0:C], v_hi[:, x, 0:C],
                                      ALU.subtract).then_inc(v_lo_ready, 1)

            def setup():
                dve.sem_inc(out_ready, 1)
                dve.memset(ones[:, :], 1.0)
                dve.memset(v_hi[:, :, C:VW].bitcast(F32), 1.0)
                dve.memset(wv_hi[:, :, C + 1:VW].bitcast(F32), 0.0)
                dve.memset(wv_lo[:, :, C + 1:VW].bitcast(F32), 0.0)
                for c in range(NC):
                    stats_x(0, QT * c, QT)
                    moments_x(0, c)
                for r in range(QT):
                    h0_split(0, r)

            def weights_step(s):
                if s == 1:
                    dve.wait_ge(biases_in, 4 * 16)
                    dve.wait_ge(weights_in, 4 * 16)
                    dve.tensor_tensor(bprod[:, :], bqk[:, 0], bqk[:, 1], ALU.mult).then_inc(bprod_ready, 1)
                    link(dve.tensor_copy(w_hi[:, :, :], w_f))
                    dve.tensor_tensor(w_lo[:, :, :], w_f, w_hi[:, :, :], ALU.subtract)
                if s in (5, 6):
                    k = s - 5
                    dve.wait_ge(setup_pe, 1)
                    link(dve.tensor_copy(m_hi[:, k], att[:, k, 0:C]))
                    dve.tensor_tensor(m_lo[:, k], att[:, k, 0:C], m_hi[:, k], ALU.subtract)
                    link(dve.tensor_copy(wv_hi[:, k, 0:C + 1], att[:, CH + k, 0:C + 1]))
                    dve.tensor_tensor(wv_lo[:, k, 0:C + 1], att[:, CH + k, 0:C + 1],
                                      wv_hi[:, k, 0:C + 1], ALU.subtract)
                if s == 6:
                    link(dve.tensor_copy(bz[:, :], att[:, 0, C:C + CH]))
                    dve.tensor_copy(s0[:, :], att[:, 0, C + CH:C + CH + 1]).then_inc(weights_ready, 1)
                    dve.wait_ge(weights_ready, 1)

            def step(i, s, layer1, layer0, after, before):
                b, a = i, i + 1
                c, t = s // KT, s % KT
                side = side_steps(i, s, layer1, layer0)
                end = end_steps(i, s, layer1, layer0)
                spare = bank_t if layer1 or not layer0 else bank_s
                if s == 4 and layer1:
                    operation_lo(("h", b, 2), bank_t)
                    operation_lo(("h", b, 3), bank_s)
                    operation_lo(("z", b, 2), bank_t)
                    operation_lo(("z", b, 3), bank_s)
                    operation_lo(("v", b, 4), bank_t)
                if side and s in (5, 12):
                    operation_lo(side, spare)
                if layer1:
                    dve.wait_ge(exp_ready, nth(TILES, b, s))
                    dve.wait_ge(a_t_ready, nth(TILES, b, s))
                    dve.wait_ge(p_lo_ready, nth(TILES, b, s - 1))
                    dve.tensor_tensor(pf[:, :], score_bank(s, layer0), a_t[:, c, t], ALU.mult).then_inc(p_ready, 1)
                if side and s not in (5, 12):
                    operation_lo(side, spare)
                norm = norm_steps(i, s, layer1, layer0)
                if s in (7, 11, 13, 14) and after:
                    stats_x(a + 1, {7: 0, 11: 2, 13: 4, 14: 6}[s], 2)
                if norm:
                    n, cc, pair = norm
                    dve.wait_ge(y_done, nth(4, n, 2 * cc + pair))
                    dve.wait_ge(rinv0_ready, nth(NC, n, cc))
                    dve.wait_ge(xb_ready, nth(NC, n, cc))
                    if pair == 0:
                        dve.wait_ge(half_out_ready, nth(NC, n - 1, cc))
                    else:
                        dve.wait_ge(out_ready, nth(NC, n - 1, cc + 1))
                    for k in range(2):
                        r = 2 * pair + k
                        ins = dve.scalar_tensor_tensor(x1[:, QT * cc + r], bank_t[:, C * k:C * k + C],
                                                       rinv0[:, r:r + 1], xb[:, QT * cc + r],
                                                       ALU.mult, ALU.add)
                    ins.then_inc(x1_ready, 1)
                if layer1:
                    dve.wait_ge(p_ready, nth(TILES, b, s))
                    dve.tensor_copy(p_hi[:, s % 2], pf[:, :]).then_inc(p_hi_ready, 1)
                if norm:
                    dve.wait_ge(x1_ready, nth(4, n, 2 * cc + pair))
                    for k in range(2):
                        dve.bn_stats(st1[:, k], x1[:, QT * cc + 2 * pair + k]).then_inc(bn1, 1)
                    dve.wait_ge(bn1, nth(KT, n, QT * cc + 2 * pair + 1))
                if layer1:
                    dve.wait_ge(p_hi_ready, nth(TILES, b, s))
                    dve.tensor_tensor(p_lo[:, s % 2], pf[:, :], p_hi[:, s % 2],
                                      ALU.subtract).then_inc(p_lo_ready, 1)
                if t == 0 and (layer0 if c else layer1):
                    n = a if c else b
                    for k in range(CH):
                        dve.wait_ge(g_hi_ready, nth(4, n, 2 * (1 - c) + k))
                        dve.tensor_tensor(g_lo[:, k], agg[:, k], g_hi[:, k],
                                          ALU.subtract).then_inc(g_lo_ready, 1)
                if norm:
                    n, cc, pair = norm
                    for k in range(2):
                        dve.bn_aggr(mv1[:, pair, k], st1[:, k]).then_inc(mv1_ready, 1)
                    dve.wait_ge(mv1_ready, nth(KT, n, QT * cc + 2 * pair + 1))
                    dve.tensor_scalar(ve1[:, pair], mv1[:, pair, :, 1], EPS, None, ALU.add)
                    dve.tensor_scalar(nm1[:, pair], mv1[:, pair, :, 0], -1.0, None,
                                      ALU.mult).then_inc(st1_ready, 1)
                if t == 0 and (before if c == 0 else layer1):
                    ob, oc = (b, 0) if c else (b - 1, 1)
                    dve.wait_ge(pv_done, nth(TILES, ob, (s - 1) % TILES))
                    dve.wait_ge(half_att_read, nth(NC, ob, oc - 1))
                    dve.reciprocal(rinv1[:, :], att[:, :, C]).then_inc(rinv1_ready, 1)
                    dve.wait_ge(rinv1_ready, nth(NC, ob, oc))
                if t == 0 and (layer0 if c else layer1):
                    n = a if c else b
                    dve.wait_ge(rsum_ready, nth(TILES, n, (s - 1) % TILES))
                    dve.tensor_tensor(rsum2[:, :], rsum[:, 1 - c, 0], rsum[:, 1 - c, 1], ALU.add).then_inc(rsum2_ready, 1)
                    dve.wait_ge(rsum2_ready, nth(NC, n, 1 - c))
                    dve.reciprocal(rinv0[:, :], rsum2[:, :]).then_inc(rinv0_ready, 1)
                if layer0:
                    dve.wait_ge(a_hi_ready, nth(TILES, a, s))
                    dve.tensor_tensor(a_lo[:, s % 2], a_t[:, c, t], a_hi[:, s % 2],
                                      ALU.subtract).then_inc(a_lo_ready, 1)
                if end:
                    operation_lo(end, spare)
                if t == 0 and (before if c == 0 else layer1):
                    dve.wait_ge(x1b_ready, nth(4, ob, 2 * oc + 1))
                    dve.wait_ge(stored, nth(NC, ob, oc, 16))
                    for r in range(2):
                        ins = dve.scalar_tensor_tensor(o_sb[:, r], att[:, r, 0:C], rinv1[:, r:r + 1],
                                                       x1[:, QT * oc + r], ALU.mult, ALU.add)
                    ins.then_inc(half_out_ready, 1)
                if s in (11, 14) and after:
                    moments_x(a + 1, 0 if s == 11 else 1)
                for h0 in h0_steps(i, s, layer0, after):
                    h0_split(*h0)
                if layer0 and not layer1:
                    weights_step(s)

            turns(dve, step, setup)

        @block.tensor
        def _(pe):
            def three(dst, l_hi, l_lo, r_hi, r_lo, start, stop):
                n = r_lo.shape[-1]
                pe.matmul(dst, l_hi, r_hi, start=start, stop=False)
                pe.matmul(dst[:, 0:n], l_hi, r_lo, start=False, stop=False)
                return pe.matmul(dst, l_lo, r_hi, start=False, stop=stop)

            def setup():
                pe.wait_ge(ident_ready, 1)

            def weight_products():
                pe.wait_ge(bprod_ready, 1)
                pe.wait_ge(biases_in, 4 * 16)
                pe.wait_ge(weights_in, 4 * 16)
                for k in range(CH):
                    ch = slice(P * k, P * k + P)
                    for o in range(CH):
                        pe.matmul(att[:, k, 0:C], wk_f[:, o, ch], wq_f[:, o, :],
                                  start=(o == 0), stop=(o == CH - 1))
                    for o in range(CH):
                        pe.transpose(att[:, CH + k, P * o:P * o + P], wv_f[:, o, ch], ident[:, :])
                    for o in range(CH):
                        pe.matmul(att[:, CH + k, C:C + 1], wk_f[:, o, ch], bqk[:, 0, o:o + 1],
                                  start=(o == 0), stop=(o == CH - 1))
                for k in range(CH):
                    for o in range(CH):
                        pe.matmul(att[:, 0, C + k:C + k + 1], wq_f[:, o, P * k:P * k + P],
                                  bqk[:, 1, o:o + 1], start=(o == 0), stop=(o == CH - 1))
                for o in range(CH):
                    mm = pe.matmul(att[:, 0, C + CH:C + CH + 1], ones[:, :], bprod[:, o:o + 1],
                                   start=(o == 0), stop=(o == CH - 1))
                mm.then_inc(setup_pe, 1)

            def step(i, s, layer1, layer0, after, before):
                b, a = i, i + 1
                c, t = s // KT, s % KT

                first = layer0 and not layer1
                spare = bank_s if first else bank_t
                lo_ready = {"h": ht_lo_ready, "z": z_lo_ready, "v": v_lo_ready}

                def bank_t_free_before():
                    if end_before and not (first or s == 0 and not before):
                        kind, n, x = end_before
                        pe.wait_ge(lo_ready[kind], nth(EVENTS[kind], n, x))
                    elif s == 0:
                        pe.wait_ge(a_t_ready, nth(TILES, b, TILES - 1))
                    elif layer0:
                        pe.wait_ge(a_t_ready, nth(TILES, a, s - 1))

                def scores():
                    if s == 4:
                        pe.wait_ge(z_lo_ready, nth(4, b, 3))
                    elif s > 0:
                        pe.wait_ge(p_ready, nth(TILES, b, s - (1 if layer0 or s < 3 else 2)))
                    elif before:
                        pe.wait_ge(p_ready, nth(TILES, b - 1, TILES - 1))
                    else:
                        pe.wait_ge(v_lo_ready, nth(KT, b, 2))
                    for k in range(CH):
                        mm = three(score_bank(s, layer0),
                                   z_hi[:, k, P * t:P * t + P], z_lo[:, k, P * t:P * t + P],
                                   ht_hi[:, k, Q * c:Q * c + Q], ht_lo[:, k, Q * c:Q * c + Q],
                                   k == 0, k == CH - 1)
                    mm.then_inc(s_done, 1)

                def aggregate(n, tile, halves):
                    m = tile % KT
                    if m == 0:
                        pe.wait_ge(g_lo_ready, nth(4, n, 4 * (tile // KT) // 2 - 1))
                    if tile < KT:
                        pe.wait_ge(h0_ready, nth(KT, n, m))
                    pe.wait_ge(a_lo_ready, nth(TILES, n, tile))
                    for k in halves:
                        ch = slice(P * k, P * k + P)
                        mm = three(agg[:, k], h0_hi[:, m, ch], h0_lo[:, m, ch],
                                   a_hi[:, tile % 2], a_lo[:, tile % 2], m == 0, m == KT - 1)
                    if k == CH - 1:
                        mm.then_inc(ah_done, 1)

                def transposes():
                    if t % QT == 0:
                        pe.wait_ge(rows_in[t // QT], nth(NC, a, c, 16))
                    if norm:
                        pe.wait_ge(x1_ready, nth(4, norm[0], 2 * norm[1] + norm[2]))
                    elif side and not first:
                        kind, n, x = side
                        pe.wait_ge(lo_ready[kind], nth(EVENTS[kind], n, x))
                    elif s == 4 and layer1:
                        pe.wait_ge(v_lo_ready, nth(KT, b, 4))
                    else:
                        bank_t_free_before()
                    h, m = t // QT, t % QT
                    for r in range(QT):
                        mm = pe.transpose(bank_t[:, P * r:P * r + P], rows[:, h, r, P * m:P * m + P],
                                          ident[:, :])
                    mm.then_inc(tr_done, 1)

                def values(n, tile, row_tiles):
                    kt = tile % KT
                    if kt == 0:
                        pe.wait_ge(half_out_ready, nth(NC, n, tile // KT - 1))
                        pe.wait_ge(half_att_read, nth(NC, n, tile // KT - 1))
                    pe.wait_ge(v_lo_ready, nth(KT, n, kt))
                    pe.wait_ge(p_lo_ready, nth(TILES, n, tile))
                    for r in row_tiles:
                        q = slice(P * r, P * r + P)
                        mm = three(att[:, r, 0:VW], p_hi[:, tile % 2, q], p_lo[:, tile % 2, q],
                                   v_hi[:, kt], v_lo[:, kt], kt == 0, kt == KT - 1)
                    if r == QT - 1:
                        mm.then_inc(pv_done, 1)

                def y_pair(n, cc, pair):
                    if first:
                        pe.wait_ge(weights_ready, 1)
                    pe.wait_ge(g_lo_ready, nth(4, n, 2 * cc + 1))
                    if pair and not layer0:
                        pe.wait_ge(x1_ready, nth(4, n, 2 * cc))
                    else:
                        bank_t_free_before()
                    for r in range(2):
                        q = slice(P * (2 * pair + r), P * (2 * pair + r) + P)
                        for k in range(CH):
                            mm = three(bank_t[:, C * r:C * r + C], g_hi[:, k, q], g_lo[:, k, q],
                                       w_hi[:, k], w_lo[:, k], k == 0, k == CH - 1)
                    mm.then_inc(y_done, 1)

                def operation(op, bank):
                    kind, n, x = op
                    cols = slice(Q * (x // 2), Q * (x // 2) + Q)
                    if kind == "h":
                        pe.wait_ge(h1_ready, nth(KT, n, QT * (x // 2) + QT - 1))
                        for r in range(QT):
                            mm = pe.transpose(bank[:, P * r:P * r + P],
                                              h1[:, r, P * (x % 2):P * (x % 2) + P], ident[:, :])
                        mm.then_inc(ht_done, 1)
                    elif kind == "z":
                        dd = slice(P * (x % 2), P * (x % 2) + P)
                        for k in range(CH):
                            pe.wait_ge(ht_lo_ready, nth(4, n, 2 * (x // 2) + k))
                            mm = three(bank[:, :], m_hi[:, k, dd], m_lo[:, k, dd],
                                       ht_hi[:, k, cols], ht_lo[:, k, cols], k == 0, k == CH - 1)
                        mm.then_inc(z_done, 1)
                    else:
                        rows_x = slice(P * x, P * x + P)
                        for k in range(CH):
                            mm = three(bank[:, 0:VW], ht_hi[:, k, rows_x], ht_lo[:, k, rows_x],
                                       wv_hi[:, k], wv_lo[:, k], k == 0, k == CH - 1)
                        mm.then_inc(v_done, 1)

                norm = norm_steps(i, s, layer1, layer0)
                side = side_steps(i, s, layer1, layer0)
                end = end_steps(i, s, layer1, layer0)
                end_before = (end_steps(i, s - 1, layer1, layer0) if s else
                              end_steps(i - 1, TILES - 1, layer1, layer1))
                late = (b - 1, TILES - 1) if s == 0 else (b, s - 1)
                has_late = before if s == 0 else layer1
                agg_of = (b, TILES - 1) if s == 0 else (a, s - 1)
                has_agg = layer1 if s == 0 else layer0
                if s == 4 and layer1:
                    if layer0:
                        pe.wait_ge(a_t_ready, nth(TILES, a, s - 1))
                    operation(("h", b, 2), bank_t)
                    pe.wait_ge(p_ready, nth(TILES, b, s - (1 if layer0 else 2)))
                    operation(("h", b, 3), bank_s)
                    values(*late, range(QT - 1))
                    operation(("z", b, 2), bank_t)
                    operation(("z", b, 3), bank_s)
                    if has_agg:
                        aggregate(*agg_of, range(1))
                    pe.wait_ge(z_lo_ready, nth(4, b, 2))
                    operation(("v", b, 4), bank_t)
                    scores()
                    if has_agg:
                        aggregate(*agg_of, range(1, CH))
                    if layer0:
                        transposes()
                    values(*late, range(QT - 1, QT))
                    return
                if layer1:
                    scores()
                if side and not first:
                    if s == 5 and not layer0:
                        pe.wait_ge(v_lo_ready, nth(KT, b, 4))
                    else:
                        bank_t_free_before()
                    operation(side, spare)
                if norm:
                    y_pair(*norm)
                early = first and not norm
                ahead = (QT if norm[2] == 0 else 1) if norm else 1 if side else 0
                behind = 1 if end else 0
                if layer0 and early:
                    transposes()
                if side and first:
                    pe.wait_ge(lo_ready[side[0]], nth(4, side[1], 0))
                    operation(side, spare)
                if has_agg:
                    aggregate(*agg_of, range(CH))
                if has_late and ahead:
                    values(*late, range(ahead))
                if layer0 and not early:
                    transposes()
                if has_late and ahead < QT:
                    values(*late, range(ahead, QT - behind))
                if end:
                    kind, n, x = end
                    if layer0 and not first:
                        pe.wait_ge(a_t_ready, nth(TILES, a, s))
                    elif kind == "z":
                        pe.wait_ge(ht_lo_ready, nth(4, n, 1))
                    elif kind == "v" and x == 0:
                        pe.wait_ge(z_lo_ready, nth(4, n, 1))
                    elif kind == "v":
                        pe.wait_ge(v_lo_ready, nth(KT, n, x - 1))
                    operation(end, spare)
                    if has_late:
                        values(*late, range(QT - behind, QT))
                if first and s == 3:
                    weight_products()

            turns(pe, step, setup)


_INS = ["x", "adj", "L0_gnn_W", "L0_gnn_b", "L1_gnn_Wq_w", "L1_gnn_Wq_b", "L1_gnn_Wk_w",
        "L1_gnn_Wk_b", "L1_gnn_Wv_w", "L1_gnn_Wv_b"]


def kernel(**inputs):
    import numpy as _np
    import concourse.bacc as _bacc
    from concourse.bass_utils import run_bass_kernel_spmd as _run

    nc = _bacc.Bacc("TRN2", target_bir_lowering=False, num_devices=1)
    arrays, args = {}, []
    for name in _INS:
        a = _np.ascontiguousarray(inputs[name])
        arrays[f"in_{name}_dram"] = a
        args.append(nc.dram_tensor(f"in_{name}_dram", a.shape, mybir.dt.from_np(a.dtype),
                                   kind="ExternalInput").ap())
    out = nc.dram_tensor("out_dram", inputs["x"].shape, F32, kind="ExternalOutput").ap()
    build(nc, *args, out)
    r = _run(nc, [arrays], core_ids=[0])
    return r.results[0]["out_dram"]
```

```python
import concourse.bass as bass
from concourse import mybir
from contextlib import ExitStack

F32 = mybir.dt.float32
F32R = mybir.dt.float32r
ALU = mybir.AluOpType
ACT = mybir.ActivationFunctionType
AX = mybir.AxisListType

P = 128
EPS = 1e-5


def build(nc, x, adj, w0, b0, wq, bq, wk, bk, wv, bv, out):
    B, N, C = x.shape
    CH = C // P
    Q = 512
    NC = N // Q
    KT = N // P
    QT = Q // P
    TILES = NC * KT
    MH = N // Q
    VW = C + 2
    assert (CH, NC, KT, QT, TILES, MH) == (2, 2, 8, 4, 16, 2)
    LOOPS = B - 2

    adj_v = adj.rearrange("b (c r p) (h m) -> b c h p r m", c=NC, p=P, h=MH)
    x_v = x.rearrange("b (r p) d -> b p r d", p=P)
    out_v = out.rearrange("b (c r p) d -> b c p r d", c=NC, p=P)

    with ExitStack() as ctx:
        def sb(name, shape, dt=F32):
            return ctx.enter_context(nc.sbuf_tensor(name, shape, dt))

        def ps(name, shape):
            return ctx.enter_context(nc.psum_tensor(name, shape, F32))

        def sem(name):
            return ctx.enter_context(nc.semaphore(name))

        rows = sb("rows", [P, MH, QT, Q])
        a_t = sb("a_t", [P, NC, KT, Q])
        a_hi = sb("a_hi", [P, 2, Q], F32R)
        a_lo = sb("a_lo", [P, 2, Q], F32R)
        x_in = sb("x_in", [P, KT, C])
        xb = sb("xb", [P, KT, C])
        hf = sb("hf", [P, 2, C])
        h0_hi = sb("h0_hi", [P, KT, C], F32R)
        h0_lo = sb("h0_lo", [P, KT, C], F32R)
        g_hi = sb("g_hi", [P, CH, Q], F32R)
        g_lo = sb("g_lo", [P, CH, Q], F32R)
        scrap = sb("scrap", [P, Q])
        rsum = sb("rsum", [P, NC, MH, QT])
        rsum2 = sb("rsum2", [P, QT])
        rinv0 = sb("rinv0", [P, QT])
        x1 = sb("x1", [P, KT, C])
        h1 = sb("h1", [P, QT, C])
        ht_hi = sb("ht_hi", [P, CH, N], F32R)
        ht_lo = sb("ht_lo", [P, CH, N], F32R)
        z_hi = sb("z_hi", [P, CH, N], F32R)
        z_lo = sb("z_lo", [P, CH, N], F32R)
        v_hi = sb("v_hi", [P, KT, VW], F32R)
        v_lo = sb("v_lo", [P, KT, C], F32R)
        gk = sb("gk", [P, KT])
        pf = sb("pf", [P, Q])
        p_hi = sb("p_hi", [P, 2, Q], F32R)
        p_lo = sb("p_lo", [P, 2, Q], F32R)
        rinv1 = sb("rinv1", [P, QT])
        o_sb = sb("o_sb", [P, QT, C])
        st0 = sb("st0", [P, QT, 6])
        mv0 = sb("mv0", [P, NC, QT, 2])
        ve0 = sb("ve0", [P, NC, QT])
        nm0 = sb("nm0", [P, NC, QT])
        rstd0 = sb("rstd0", [P, NC, QT])
        nmr0 = sb("nmr0", [P, NC, QT])
        st1 = sb("st1", [P, 2, 6])
        mv1 = sb("mv1", [P, 2, 2, 2])
        ve1 = sb("ve1", [P, 2, 2])
        nm1 = sb("nm1", [P, 2, 2])
        rstd1 = sb("rstd1", [P, 2, 2])
        nmr1 = sb("nmr1", [P, 2, 2])
        ident = sb("ident", [P, P])
        ones = sb("ones", [P, P])
        mhalf = sb("mhalf", [P, QT])
        w_hi = sb("w_hi", [P, CH, C], F32R)
        w_lo = sb("w_lo", [P, CH, C], F32R)
        m_hi = sb("m_hi", [P, CH, C], F32R)
        m_lo = sb("m_lo", [P, CH, C], F32R)
        wv_hi = sb("wv_hi", [P, CH, VW], F32R)
        wv_lo = sb("wv_lo", [P, CH, VW], F32R)
        b0_all = sb("b0_all", [P, C])
        bv_all = sb("bv_all", [P, C])
        bqk = sb("bqk", [P, 2, CH])
        bprod = sb("bprod", [P, CH])
        bz = sb("bz", [P, CH])
        s0 = sb("s0", [P, 1])
        w_f = x1[:, 0:CH, :]
        wq_f = x1[:, CH:2 * CH, :]
        wk_f = x1[:, 2 * CH:3 * CH, :]
        wv_f = x1[:, 3 * CH:4 * CH, :]

        bank_t = ps("bank_t", [P, Q])
        bank_s = ps("bank_s", [P, Q])
        agg = ps("agg", [P, CH, Q])
        att = ps("att", [P, QT, Q])

        rows_in = [sem(f"rows_in{h}") for h in range(MH)]
        x_got = [sem(f"x_got{c}") for c in range(NC)]
        weights_in = sem("weights_in")
        biases_in = sem("biases_in")
        stored = sem("stored")
        ident_zero = sem("ident_zero")
        ident_ready = sem("ident_ready")
        bprod_ready = sem("bprod_ready")
        setup_pe = sem("setup_pe")
        setup_dve = sem("setup_dve")
        weights_ready = sem("weights_ready")
        tr_done = sem("tr_done")
        ah_done = sem("ah_done")
        y_done = sem("y_done")
        ht_done = sem("ht_done")
        z_done = sem("z_done")
        v_done = sem("v_done")
        s_done = sem("s_done")
        pv_done = sem("pv_done")
        a_hi_ready = sem("a_hi_ready")
        a_t_ready = sem("a_t_ready")
        rsum_ready = sem("rsum_ready")
        exp_ready = sem("exp_ready")
        g_hi_ready = sem("g_hi_ready")
        ht_hi_ready = sem("ht_hi_ready")
        z_hi_ready = sem("z_hi_ready")
        v_hi_ready = sem("v_hi_ready")
        hf_ready = sem("hf_ready")
        h1_ready = sem("h1_ready")
        half_att_read = sem("half_att_read")
        a_lo_ready = sem("a_lo_ready")
        p_ready = sem("p_ready")
        p_hi_ready = sem("p_hi_ready")
        p_lo_ready = sem("p_lo_ready")
        g_lo_ready = sem("g_lo_ready")
        rsum2_ready = sem("rsum2_ready")
        rinv0_ready = sem("rinv0_ready")
        ht_lo_ready = sem("ht_lo_ready")
        z_lo_ready = sem("z_lo_ready")
        v_lo_ready = sem("v_lo_ready")
        gk_ready = sem("gk_ready")
        h0_hi_ready = sem("h0_hi_ready")
        h0_ready = sem("h0_ready")
        x1_ready = sem("x1_ready")
        x1_tile = sem("x1_tile")
        bn0 = sem("bn0")
        mv0_ready = sem("mv0_ready")
        st0_ready = sem("st0_ready")
        bn1 = sem("bn1")
        mv1_ready = sem("mv1_ready")
        st1_ready = sem("st1_ready")
        rinv1_ready = sem("rinv1_ready")
        half_out_ready = sem("half_out_ready")
        out_ready = sem("out_ready")
        pow0 = sem("pow0")
        ln0_ready = sem("ln0_ready")
        pow1 = sem("pow1")
        ln1_ready = sem("ln1_ready")
        xb_ready = sem("xb_ready")
        x1b_ready = sem("x1b_ready")

        def nth(per, batch, n, by=1):
            value = (batch * per + (n + 1)) * by
            return max(value, 0) if isinstance(value, int) else value

        def turns(eng, step, setup):
            setup()
            for s in range(TILES):
                step(-1, s, False, True, True, False)
            for s in range(2):
                step(0, s, True, True, True, False)
            with eng.Fori(0, LOOPS) as i:
                for s in range(2, TILES):
                    step(i, s, True, True, True, True)
                for s in range(2):
                    step(i + 1, s, True, True, True, True)
            for s in range(2, TILES):
                step(B - 2, s, True, True, False, True)
            for s in range(2):
                step(B - 1, s, True, False, False, True)
            for s in range(2, TILES):
                step(B - 1, s, True, False, False, True)
            for s in range(2):
                step(B, s, False, False, False, True)

        def norm_steps(i, s, layer1, layer0):
            if s in (1, 2) and layer1:
                return i, 1, s - 1
            if s in (9, 10) and layer0:
                return i + 1, 0, s - 9
            return None

        def relu_steps(i, s, layer1, layer0):
            return norm_steps(i, s - 1, layer1, layer0)

        def side_steps(i, s, layer1, layer0):
            if s in (13, 14, 15) and layer0:
                return "v", i + 1, s - 13
            if s in (0, 5) and layer1:
                return "v", i, 3 if s == 0 else 5
            return None

        def end_steps(i, s, layer1, layer0):
            if s in (11, 12) and layer0:
                return "h", i + 1, s - 11
            if s in (13, 14) and layer0:
                return "z", i + 1, s - 13
            if s in (5, 6) and layer1:
                return "v", i, s + 1
            return None

        def h0_steps(i, s, layer1, layer0, after):
            if s >= 12 and after:
                return [(i + 2, s - 12)]
            if not layer1 and layer0:
                return [(i + 1, s + 2 if s < 2 else s + 1)] if s < 7 and s != 2 else []
            if s in (2, 4) and layer0:
                return [(i + 1, 3 + s // 2)]
            if s == 5 and layer0:
                return [(i + 1, 6), (i + 1, 7)]
            return []

        def op_bank(op, first):
            kind, n, x = op
            return att[:, x % 2 + (2 if kind == "z" else 0) if kind != "v" else x] if first else bank_t

        def score_bank(s, layer0):
            return agg[:, 0] if not layer0 and s >= 3 and s % 2 else bank_s[:, :]

        EVENTS = {"h": 4, "z": 4, "v": KT}

        block = ctx.enter_context(nc.Block())

        @block.sync
        def _(sp):
            def load_rows(a, c, h):
                sp.dma_start(rows[:, h], adj_v[a, c, h]).then_inc(rows_in[h], 16)

            def load_x(a, c):
                half = slice(QT * c, QT * c + QT)
                sp.dma_start(x_in[:, half], x_v[a][:, half]).then_inc(x_got[c], 16)

            def setup():
                sp.sem_inc(stored, 16)
                load_x(0, 0)
                load_rows(0, 0, 0)
                load_x(0, 1)
                sp.dma_start(b0_all[:, :], b0.rearrange("(a d) -> a d", a=1)
                             .to_broadcast([P, C])).then_inc(biases_in, 16)
                sp.dma_start(bv_all[:, :], bv.rearrange("(a d) -> a d", a=1)
                             .to_broadcast([P, C])).then_inc(biases_in, 16)
                with nc.allow_non_contiguous_dma(reason="two vectors of 256 down the partitions"):
                    sp.dma_start(bqk[:, 0], bq.rearrange("(t p) -> p t", p=P)).then_inc(biases_in, 16)
                    sp.dma_start(bqk[:, 1], bk.rearrange("(t p) -> p t", p=P)).then_inc(biases_in, 16)
                for dst, src in ((w_f, w0), (wq_f, wq), (wk_f, wk), (wv_f, wv)):
                    sp.dma_start(dst, src.rearrange("(t p) d -> p t d", p=P)).then_inc(weights_in, 16)
                load_rows(0, 0, 1)

            def step(i, s, layer1, layer0, after, before):
                b, a = i, i + 1
                c, t = s // KT, s % KT
                if s == 5 and after:
                    sp.wait_ge(xb_ready, nth(NC, a, 1))
                    sp.wait_ge(hf_ready, nth(KT, a, KT - 1))
                    load_x(a + 1, 0)
                    load_x(a + 1, 1)
                if t in (3, 7) and (layer0 if c == 0 else after):
                    sp.wait_ge(tr_done, nth(TILES, a, s))
                    sp.wait_ge(rsum_ready, nth(TILES, a, s))
                    load_rows(a + c, 1 - c, t // QT)
                if t == 1 and (before if c == 0 else layer1):
                    ob = b - 1 if c == 0 else b
                    sp.wait_ge(out_ready, nth(NC, ob, 2 - c))
                    sp.dma_start(out_v[ob, 1 - c], o_sb[:, :, :]).then_inc(stored, 16)

            turns(sp, step, setup)
            sp.wait_ge(stored, nth(NC, B - 1, NC, 16))

        @block.gpsimd
        def _(pool):
            def add_b0(a, c):
                pool.wait_ge(x_got[c], nth(1, a, 0, 16))
                pool.wait_ge(x1_ready, nth(4, a - 1, 2 * c + 1))
                pool.tensor_tensor(xb[:, QT * c:QT * c + QT], x_in[:, QT * c:QT * c + QT],
                                   b0_all[:, None, :].to_broadcast([P, QT, C]),
                                   ALU.add).then_inc(xb_ready, 1)

            def rstd_x(a, c):
                pool.wait_ge(st0_ready, nth(NC, a, c))
                pool.wait_ge(hf_ready, nth(KT, a - 1, QT * c + QT - 1))
                pool.tensor_tensor(rstd0[:, c], ve0[:, c], mhalf[:, 0:QT], ALU.pow).then_inc(pow0, 1)
                pool.wait_ge(pow0, nth(NC, a, c))
                pool.tensor_tensor(nmr0[:, c], nm0[:, c], rstd0[:, c], ALU.mult).then_inc(ln0_ready, 1)

            def setup():
                pool.memset(ident[:, :], 0.0).then_inc(ident_zero, 1)
                pool.memset(mhalf[:, :], -0.5)
                pool.wait_ge(ident_zero, 1)
                pool.affine_select(out=ident[:, :], in_=ident[:, :], compare_op=ALU.not_equal,
                                   fill=1.0, base=0, pattern=[[-1, P]],
                                   channel_multiplier=1).then_inc(ident_ready, 1)
                pool.wait_ge(ident_ready, 1)
                rstd_x(0, 0)
                rstd_x(0, 1)
                pool.wait_ge(biases_in, 4 * 16)
                add_b0(0, 0)

            def step(i, s, layer1, layer0, after, before):
                b, a = i, i + 1
                c, t = s // KT, s % KT
                if t == 1 and (before if c == 0 else layer1):
                    ob, oc = (b, 0) if c else (b - 1, 1)
                    pool.wait_ge(half_out_ready, nth(NC, ob, oc))
                    pool.wait_ge(half_att_read, nth(NC, ob, oc))
                    pool.wait_ge(x1b_ready, nth(4, ob, 2 * oc + 1))
                    pool.tensor_tensor(o_sb[:, 2:QT], o_sb[:, 2:QT], x1[:, QT * oc + 2:QT * oc + QT],
                                       ALU.add).then_inc(out_ready, 1)
                if s in (11, 15) and after:
                    rstd_x(a + 1, 0 if s == 11 else 1)
                ready = relu_steps(i, s - 1, layer1, layer0)
                if ready:
                    n, c, pair = ready
                    r = QT * c + 2 * pair
                    pool.wait_ge(h1_ready, nth(KT, n, r + 1))
                    pool.tensor_tensor(x1[:, r:r + 2], x1[:, r:r + 2],
                                       bv_all[:, None, :].to_broadcast([P, 2, C]),
                                       ALU.add).then_inc(x1b_ready, 1)
                if s == 3 and layer0:
                    add_b0(a, 1)
                if s == 11 and after:
                    add_b0(a + 1, 0)
                norm = norm_steps(i, s, layer1, layer0)
                if norm:
                    n, c, pair = norm
                    pool.wait_ge(st1_ready, nth(4, n, 2 * c + pair))
                    pool.tensor_tensor(rstd1[:, pair], ve1[:, pair], mhalf[:, 0:2],
                                       ALU.pow).then_inc(pow1, 1)
                    pool.wait_ge(pow1, nth(4, n, 2 * c + pair))
                    pool.tensor_tensor(nmr1[:, pair], nm1[:, pair], rstd1[:, pair],
                                       ALU.mult).then_inc(ln1_ready, 1)

            turns(pool, step, setup)

        @block.scalar
        def _(act):
            def h0_relu(a, r):
                act.wait_ge(ln0_ready, nth(NC, a, r // QT))
                act.wait_ge(h0_ready, nth(KT, a, r - 2))
                act.activation(hf[:, r % 2], x_in[:, r], ACT.Relu,
                               bias=nmr0[:, r // QT, r % QT:r % QT + 1],
                               scale=rstd0[:, r // QT, r % QT:r % QT + 1]).then_inc(hf_ready, 1)

            def row_sums(a, s):
                c, t = s // KT, s % KT
                if t % QT == 0:
                    act.wait_ge(rows_in[t // QT], nth(NC, a, c, 16))
                if t == 0:
                    act.wait_ge(rsum2_ready, nth(NC, a - 1, c))
                act.wait_ge(rsum_ready, nth(TILES, a, s - 1))
                act.activation(scrap[:, :], rows[:, t // QT, t % QT], ACT.Copy,
                               accum_out=rsum[:, c, t // QT, t % QT:t % QT + 1]).then_inc(rsum_ready, 1)

            def tile_of_a(a, s):
                act.wait_ge(tr_done, nth(TILES, a, s))
                act.activation(a_t[:, s // KT, s % KT], bank_t[:, :], ACT.Copy).then_inc(a_t_ready, 1)

            def h1_relu(n, cc, pair):
                act.wait_ge(ln1_ready, nth(4, n, 2 * cc + pair))
                if pair == 0:
                    act.wait_ge(ht_done, nth(4, n, 2 * cc - 1))
                for k in range(2):
                    r = 2 * pair + k
                    act.activation(h1[:, r], x1[:, QT * cc + r], ACT.Relu,
                                   bias=nmr1[:, pair, k:k + 1],
                                   scale=rstd1[:, pair, k:k + 1]).then_inc(h1_ready, 1)

            def operation_hi(op, bank):
                kind, n, x = op
                cols = slice(Q * (x // 2), Q * (x // 2) + Q)
                if kind == "h":
                    act.wait_ge(ht_done, nth(4, n, x))
                    act.activation(ht_hi[:, x % 2, cols], bank[:, :], ACT.Copy).then_inc(ht_hi_ready, 1)
                elif kind == "z":
                    act.wait_ge(z_done, nth(4, n, x))
                    act.activation(z_hi[:, x % 2, cols], bank[:, :], ACT.Identity,
                                   bias=bz[:, x % 2:x % 2 + 1]).then_inc(z_hi_ready, 1)
                else:
                    act.wait_ge(v_done, nth(KT, n, x))
                    act.activation(v_hi[:, x, 0:C], bank[:, 0:C], ACT.Copy).then_inc(v_hi_ready, 1)

            def setup():
                for r in range(2):
                    h0_relu(0, r)

            def step(i, s, layer1, layer0, after, before):
                b, a = i, i + 1
                c, t = s // KT, s % KT
                side = side_steps(i, s, layer1, layer0)
                end = end_steps(i, s, layer1, layer0)
                first = layer0 and not layer1
                if first:
                    tile_of_a(a, s)
                if s == 4 and layer1:
                    operation_hi(("h", b, 2), bank_t)
                    operation_hi(("h", b, 3), bank_s)
                    if layer0:
                        row_sums(a, s - 2)
                        row_sums(a, s - 1)
                    operation_hi(("z", b, 2), bank_t)
                    operation_hi(("z", b, 3), bank_s)
                    operation_hi(("v", b, 4), bank_t)
                if side and s == 5:
                    operation_hi(side, op_bank(side, first))
                if layer1:
                    act.wait_ge(s_done, nth(TILES, b, s))
                    if c == 0:
                        act.wait_ge(gk_ready, nth(KT, b, t))
                    act.activation(score_bank(s, layer0), score_bank(s, layer0), ACT.Exp,
                                   bias=gk[:, t:t + 1]).then_inc(exp_ready, 1)
                if side and s != 5:
                    operation_hi(side, op_bank(side, first))
                relu = relu_steps(i, s, layer1, layer0)
                if relu:
                    h1_relu(*relu)
                if s == 0 and layer1:
                    row_sums(b, TILES - 1)
                elif s > 0 and layer0 and not (s in (3, 4) and layer1):
                    row_sums(a, s - 1)
                if t == 0 and (layer0 if c else layer1):
                    n = a if c else b
                    for k in range(CH):
                        if k == 0:
                            act.wait_ge(ah_done, nth(TILES, n, (s - 1) % TILES))
                        act.activation(g_hi[:, k], agg[:, k], ACT.Copy).then_inc(g_hi_ready, 1)
                if layer0 and not first:
                    act.wait_ge(p_ready, nth(TILES, a - 1, s))
                    tile_of_a(a, s)
                    act.wait_ge(a_t_ready, nth(TILES, a, s))
                    act.activation(a_hi[:, s % 2], a_t[:, c, t], ACT.Copy).then_inc(a_hi_ready, 1)
                if t == 0 and (before if c == 0 else layer1):
                    ob, oc = (b, 0) if c else (b - 1, 1)
                    act.wait_ge(rinv1_ready, nth(NC, ob, oc))
                    act.wait_ge(stored, nth(NC, ob, oc, 16))
                    for r in range(2, QT):
                        ins = act.activation(o_sb[:, r], att[:, r, 0:C], ACT.Identity,
                                             scale=rinv1[:, r:r + 1])
                    ins.then_inc(half_att_read, 1)
                for h0 in h0_steps(i, s, layer1, layer0, after):
                    h0_relu(*h0)
                if end:
                    operation_hi(end, op_bank(end, first))

            turns(act, step, setup)

        @block.vector
        def _(dve):
            def h0_split(a, r):
                dve.wait_ge(hf_ready, nth(KT, a, r))
                dve.wait_ge(ah_done, nth(TILES, a - 1, KT + r))
                dve.tensor_copy(h0_hi[:, r], hf[:, r % 2]).then_inc(h0_hi_ready, 1)
                dve.wait_ge(h0_hi_ready, nth(KT, a, r))
                dve.tensor_tensor(h0_lo[:, r], hf[:, r % 2], h0_hi[:, r],
                                  ALU.subtract).then_inc(h0_ready, 1)

            def stats_x(a, r0, tiles):
                dve.wait_ge(x_got[r0 // QT], nth(1, a, 0, 16))
                for r in range(r0, r0 + tiles):
                    dve.bn_stats(st0[:, r % QT], x_in[:, r]).then_inc(bn0, 1)
                dve.wait_ge(bn0, nth(KT, a, r0 + tiles - 1))

            def moments_x(a, c):
                for r in range(QT):
                    dve.bn_aggr(mv0[:, c, r], st0[:, r]).then_inc(mv0_ready, 1)
                dve.wait_ge(ln0_ready, nth(NC, a - 1, c))
                dve.wait_ge(mv0_ready, nth(KT, a, QT * c + QT - 1))
                dve.tensor_scalar(ve0[:, c], mv0[:, c, :, 1], EPS, None, ALU.add)
                dve.tensor_scalar(nm0[:, c], mv0[:, c, :, 0], -1.0, None, ALU.mult).then_inc(st0_ready, 1)

            def tile_lo(a, s):
                dve.wait_ge(a_hi_ready, nth(TILES, a, s))
                dve.tensor_tensor(a_lo[:, s % 2], a_t[:, s // KT, s % KT], a_hi[:, s % 2],
                                  ALU.subtract).then_inc(a_lo_ready, 1)

            links = [0]

            def link(ins):
                links[0] += 1
                ins.then_inc(setup_dve, 1)
                dve.wait_ge(setup_dve, links[0])

            def operation_lo(op, bank):
                kind, n, x = op
                cols = slice(Q * (x // 2), Q * (x // 2) + Q)
                if kind == "h":
                    dve.wait_ge(ht_hi_ready, nth(4, n, x))
                    dve.tensor_tensor(ht_lo[:, x % 2, cols], bank[:, :], ht_hi[:, x % 2, cols],
                                      ALU.subtract).then_inc(ht_lo_ready, 1)
                elif kind == "z":
                    dve.wait_ge(z_hi_ready, nth(4, n, x))
                    dve.scalar_tensor_tensor(z_lo[:, x % 2, cols], bank[:, :], bz[:, x % 2:x % 2 + 1],
                                             z_hi[:, x % 2, cols], ALU.add,
                                             ALU.subtract).then_inc(z_lo_ready, 1)
                else:
                    dve.wait_ge(v_hi_ready, nth(KT, n, x))
                    dve.tensor_scalar(gk[:, x:x + 1], bank[:, C:C + 1], s0[:, 0:1], None,
                                      ALU.add).then_inc(gk_ready, 1)
                    dve.tensor_tensor(v_lo[:, x], bank[:, 0:C], v_hi[:, x, 0:C],
                                      ALU.subtract).then_inc(v_lo_ready, 1)

            def setup():
                dve.sem_inc(out_ready, 1)
                dve.memset(ones[:, :], 1.0)
                dve.memset(v_hi[:, :, C:VW].bitcast(F32), 1.0)
                dve.memset(wv_hi[:, :, C + 1:VW].bitcast(F32), 0.0)
                dve.memset(wv_lo[:, :, C + 1:VW].bitcast(F32), 0.0)
                stats_x(0, 0, QT)
                moments_x(0, 0)
                for r in range(2):
                    h0_split(0, r)

            def first_turn(s):
                if s in (1, 2):
                    stats_x(0, QT + 2 * (s - 1), 2)
                if s == 2:
                    moments_x(0, 1)
                if s == 3:
                    dve.wait_ge(biases_in, 4 * 16)
                    dve.wait_ge(weights_in, 4 * 16)
                    dve.tensor_tensor(bprod[:, :], bqk[:, 0], bqk[:, 1], ALU.mult).then_inc(bprod_ready, 1)
                    link(dve.tensor_copy(w_hi[:, :, :], w_f))
                    dve.tensor_tensor(w_lo[:, :, :], w_f, w_hi[:, :, :], ALU.subtract)
                if 6 <= s < 6 + 2 * CH:
                    k = (s - 6) // 2
                    dve.wait_ge(setup_pe, 1)
                    if s % 2 == 0:
                        link(dve.tensor_copy(m_hi[:, k], att[:, k, 0:C]))
                        dve.tensor_tensor(m_lo[:, k], att[:, k, 0:C], m_hi[:, k], ALU.subtract)
                    else:
                        link(dve.tensor_copy(wv_hi[:, k, 0:C + 1], att[:, CH + k, 0:C + 1]))
                        dve.tensor_tensor(wv_lo[:, k, 0:C + 1], att[:, CH + k, 0:C + 1],
                                          wv_hi[:, k, 0:C + 1], ALU.subtract)
                if s == 10:
                    link(dve.tensor_copy(bz[:, :], att[:, 0, C:C + CH]))
                    dve.tensor_copy(s0[:, :], att[:, 0, C + CH:C + CH + 1]).then_inc(weights_ready, 1)
                    dve.wait_ge(weights_ready, 1)

            def step(i, s, layer1, layer0, after, before):
                b, a = i, i + 1
                c, t = s // KT, s % KT
                side = side_steps(i, s, layer1, layer0)
                end = end_steps(i, s, layer1, layer0)
                first = layer0 and not layer1
                if first:
                    dve.wait_ge(a_t_ready, nth(TILES, a, s))
                    dve.tensor_copy(a_hi[:, s % 2], a_t[:, c, t]).then_inc(a_hi_ready, 1)
                    tile_lo(a, s)
                if s == 4 and layer1:
                    operation_lo(("h", b, 2), bank_t)
                    operation_lo(("h", b, 3), bank_s)
                    operation_lo(("z", b, 2), bank_t)
                    operation_lo(("z", b, 3), bank_s)
                    operation_lo(("v", b, 4), bank_t)
                if side and s == 5:
                    operation_lo(side, op_bank(side, first))
                if layer1:
                    dve.wait_ge(exp_ready, nth(TILES, b, s))
                    dve.wait_ge(a_t_ready, nth(TILES, b, s))
                    dve.wait_ge(p_lo_ready, nth(TILES, b, s - 1))
                    dve.tensor_tensor(pf[:, :], score_bank(s, layer0), a_t[:, c, t],
                                      ALU.mult).then_inc(p_ready, 1)
                if side and s != 5:
                    operation_lo(side, op_bank(side, first))
                norm = norm_steps(i, s, layer1, layer0)
                if s in (8 if first else 7, 11, 13, 14) and after:
                    stats_x(a + 1, {7: 0, 8: 0, 11: 2, 13: 4, 14: 6}[s], 2)
                if norm:
                    n, cc, pair = norm
                    dve.wait_ge(y_done, nth(4, n, 2 * cc + pair))
                    dve.wait_ge(rinv0_ready, nth(NC, n, cc))
                    dve.wait_ge(xb_ready, nth(NC, n, cc))
                    if pair == 0:
                        dve.wait_ge(half_out_ready, nth(NC, n - 1, cc))
                    else:
                        dve.wait_ge(out_ready, nth(NC, n - 1, cc + 1))
                    for k in range(2):
                        r = 2 * pair + k
                        y = (bank_s if first else bank_t)[:, C * k:C * k + C]
                        ins = dve.scalar_tensor_tensor(x1[:, QT * cc + r], y,
                                                       rinv0[:, r:r + 1], xb[:, QT * cc + r],
                                                       ALU.mult, ALU.add)
                    ins.then_inc(x1_ready, 1)
                if layer1:
                    if not layer0 and s > KT:
                        dve.wait_ge(pv_done, nth(TILES, b, s - 2))
                    dve.wait_ge(p_ready, nth(TILES, b, s))
                    dve.tensor_copy(p_hi[:, s % 2], pf[:, :]).then_inc(p_hi_ready, 1)
                if norm:
                    dve.wait_ge(x1_ready, nth(4, n, 2 * cc + pair))
                    for k in range(2):
                        dve.bn_stats(st1[:, k], x1[:, QT * cc + 2 * pair + k]).then_inc(bn1, 1)
                    dve.wait_ge(bn1, nth(KT, n, QT * cc + 2 * pair + 1))
                if layer1:
                    dve.wait_ge(p_hi_ready, nth(TILES, b, s))
                    dve.tensor_tensor(p_lo[:, s % 2], pf[:, :], p_hi[:, s % 2],
                                      ALU.subtract).then_inc(p_lo_ready, 1)
                if t == 0 and (layer0 if c else layer1):
                    n = a if c else b
                    for k in range(CH):
                        dve.wait_ge(g_hi_ready, nth(4, n, 2 * (1 - c) + k))
                        dve.tensor_tensor(g_lo[:, k], agg[:, k], g_hi[:, k],
                                          ALU.subtract).then_inc(g_lo_ready, 1)
                if norm:
                    n, cc, pair = norm
                    for k in range(2):
                        dve.bn_aggr(mv1[:, pair, k], st1[:, k]).then_inc(mv1_ready, 1)
                    dve.wait_ge(mv1_ready, nth(KT, n, QT * cc + 2 * pair + 1))
                    dve.tensor_scalar(ve1[:, pair], mv1[:, pair, :, 1], EPS, None, ALU.add)
                    dve.tensor_scalar(nm1[:, pair], mv1[:, pair, :, 0], -1.0, None,
                                      ALU.mult).then_inc(st1_ready, 1)
                if t == 0 and (before if c == 0 else layer1):
                    ob, oc = (b, 0) if c else (b - 1, 1)
                    dve.wait_ge(pv_done, nth(TILES, ob, (s - 1) % TILES))
                    dve.wait_ge(half_att_read, nth(NC, ob, oc - 1))
                    dve.reciprocal(rinv1[:, :], att[:, :, C]).then_inc(rinv1_ready, 1)
                    dve.wait_ge(rinv1_ready, nth(NC, ob, oc))
                if t == 0 and (layer0 if c else layer1):
                    n = a if c else b
                    dve.wait_ge(rsum_ready, nth(TILES, n, (s - 1) % TILES))
                    dve.tensor_tensor(rsum2[:, :], rsum[:, 1 - c, 0], rsum[:, 1 - c, 1],
                                      ALU.add).then_inc(rsum2_ready, 1)
                    dve.wait_ge(rsum2_ready, nth(NC, n, 1 - c))
                    dve.reciprocal(rinv0[:, :], rsum2[:, :]).then_inc(rinv0_ready, 1)
                if layer0 and not first:
                    tile_lo(a, s)
                if end:
                    operation_lo(end, op_bank(end, first))
                if t == 0 and (before if c == 0 else layer1):
                    dve.wait_ge(x1b_ready, nth(4, ob, 2 * oc + 1))
                    dve.wait_ge(stored, nth(NC, ob, oc, 16))
                    for r in range(2):
                        ins = dve.scalar_tensor_tensor(o_sb[:, r], att[:, r, 0:C], rinv1[:, r:r + 1],
                                                       x1[:, QT * oc + r], ALU.mult, ALU.add)
                    ins.then_inc(half_out_ready, 1)
                if s in (11, 15) and after:
                    moments_x(a + 1, 0 if s == 11 else 1)
                for h0 in h0_steps(i, s, layer1, layer0, after):
                    h0_split(*h0)
                if first:
                    first_turn(s)

            turns(dve, step, setup)

        @block.tensor
        def _(pe):
            def three(dst, l_hi, l_lo, r_hi, r_lo, start, stop):
                n = r_lo.shape[-1]
                pe.matmul(dst, l_hi, r_hi, start=start, stop=False)
                pe.matmul(dst[:, 0:n], l_hi, r_lo, start=False, stop=False)
                return pe.matmul(dst, l_lo, r_hi, start=False, stop=stop)

            def setup():
                pe.wait_ge(ident_ready, 1)

            def weight_products():
                pe.wait_ge(bprod_ready, 1)
                pe.wait_ge(biases_in, 4 * 16)
                pe.wait_ge(weights_in, 4 * 16)
                for k in range(CH):
                    ch = slice(P * k, P * k + P)
                    for o in range(CH):
                        pe.matmul(att[:, k, 0:C], wk_f[:, o, ch], wq_f[:, o, :],
                                  start=(o == 0), stop=(o == CH - 1))
                    for o in range(CH):
                        pe.transpose(att[:, CH + k, P * o:P * o + P], wv_f[:, o, ch], ident[:, :])
                    for o in range(CH):
                        pe.matmul(att[:, CH + k, C:C + 1], wk_f[:, o, ch], bqk[:, 0, o:o + 1],
                                  start=(o == 0), stop=(o == CH - 1))
                for k in range(CH):
                    for o in range(CH):
                        pe.matmul(att[:, 0, C + k:C + k + 1], wq_f[:, o, P * k:P * k + P],
                                  bqk[:, 1, o:o + 1], start=(o == 0), stop=(o == CH - 1))
                for o in range(CH):
                    mm = pe.matmul(att[:, 0, C + CH:C + CH + 1], ones[:, :], bprod[:, o:o + 1],
                                   start=(o == 0), stop=(o == CH - 1))
                mm.then_inc(setup_pe, 1)

            def step(i, s, layer1, layer0, after, before):
                b, a = i, i + 1
                c, t = s // KT, s % KT

                first = layer0 and not layer1
                y_bank = bank_s if first else bank_t
                lo_ready = {"h": ht_lo_ready, "z": z_lo_ready, "v": v_lo_ready}

                def bank_t_free_before():
                    if end_before and not first:
                        kind, n, x = end_before
                        pe.wait_ge(lo_ready[kind], nth(EVENTS[kind], n, x))
                    elif s == 0:
                        pe.wait_ge(a_t_ready, nth(TILES, b, TILES - 1))
                    elif layer0:
                        pe.wait_ge(a_t_ready, nth(TILES, a, s - 1))

                def scores(s):
                    if s == 4:
                        pe.wait_ge(z_lo_ready, nth(4, b, 3))
                    elif s > 0:
                        pe.wait_ge(p_ready, nth(TILES, b, s - (1 if layer0 or s < 3 else 2)))
                    elif before:
                        pe.wait_ge(p_ready, nth(TILES, b - 1, TILES - 1))
                    else:
                        pe.wait_ge(x1_ready, nth(4, b, 1))
                        pe.wait_ge(z_lo_ready, nth(4, b, 1))
                    rows_t = slice(P * (s % KT), P * (s % KT) + P)
                    for k in range(CH):
                        mm = three(score_bank(s, layer0),
                                   z_hi[:, k, rows_t], z_lo[:, k, rows_t],
                                   ht_hi[:, k, Q * c:Q * c + Q], ht_lo[:, k, Q * c:Q * c + Q],
                                   k == 0, k == CH - 1)
                    mm.then_inc(s_done, 1)

                def aggregate(n, tile, halves):
                    m = tile % KT
                    if m == 0:
                        pe.wait_ge(g_lo_ready, nth(4, n, 4 * (tile // KT) // 2 - 1))
                    if tile < KT:
                        pe.wait_ge(h0_ready, nth(KT, n, m))
                    pe.wait_ge(a_lo_ready, nth(TILES, n, tile))
                    for k in halves:
                        ch = slice(P * k, P * k + P)
                        mm = three(agg[:, k], h0_hi[:, m, ch], h0_lo[:, m, ch],
                                   a_hi[:, tile % 2], a_lo[:, tile % 2], m == 0, m == KT - 1)
                    if k == CH - 1:
                        mm.then_inc(ah_done, 1)

                def transposes():
                    if t % QT == 0:
                        pe.wait_ge(rows_in[t // QT], nth(NC, a, c, 16))
                    if norm and not first:
                        pe.wait_ge(x1_ready, nth(4, norm[0], 2 * norm[1] + norm[2]))
                    elif side and not first:
                        kind, n, x = side
                        pe.wait_ge(lo_ready[kind], nth(EVENTS[kind], n, x))
                    elif s == 4 and layer1:
                        pe.wait_ge(v_lo_ready, nth(KT, b, 4))
                    else:
                        bank_t_free_before()
                    h, m = t // QT, t % QT
                    for r in range(QT):
                        mm = pe.transpose(bank_t[:, P * r:P * r + P], rows[:, h, r, P * m:P * m + P],
                                          ident[:, :])
                    mm.then_inc(tr_done, 1)

                def values(n, tile, row_tiles):
                    kt = tile % KT
                    if kt == 0:
                        pe.wait_ge(half_out_ready, nth(NC, n, tile // KT - 1))
                        pe.wait_ge(half_att_read, nth(NC, n, tile // KT - 1))
                        if not before:
                            pe.wait_ge(v_lo_ready, nth(KT, n, 2))
                    pe.wait_ge(v_lo_ready, nth(KT, n, kt))
                    pe.wait_ge(p_lo_ready, nth(TILES, n, tile))
                    for r in row_tiles:
                        q = slice(P * r, P * r + P)
                        mm = three(att[:, r, 0:VW], p_hi[:, tile % 2, q], p_lo[:, tile % 2, q],
                                   v_hi[:, kt], v_lo[:, kt], kt == 0, kt == KT - 1)
                    if r == QT - 1:
                        mm.then_inc(pv_done, 1)

                def y_pair(n, cc, pair):
                    pe.wait_ge(g_lo_ready, nth(4, n, 2 * cc + 1))
                    if pair and not (layer0 and layer1):
                        pe.wait_ge(x1_ready, nth(4, n, 2 * cc))
                    elif not first:
                        bank_t_free_before()
                    for r in range(2):
                        q = slice(P * (2 * pair + r), P * (2 * pair + r) + P)
                        for k in range(CH):
                            mm = three(y_bank[:, C * r:C * r + C], g_hi[:, k, q], g_lo[:, k, q],
                                       w_hi[:, k], w_lo[:, k], k == 0, k == CH - 1)
                    mm.then_inc(y_done, 1)

                def operation(op, bank):
                    kind, n, x = op
                    cols = slice(Q * (x // 2), Q * (x // 2) + Q)
                    if kind == "h":
                        pe.wait_ge(h1_ready, nth(KT, n, QT * (x // 2) + QT - 1))
                        for r in range(QT):
                            mm = pe.transpose(bank[:, P * r:P * r + P],
                                              h1[:, r, P * (x % 2):P * (x % 2) + P], ident[:, :])
                        mm.then_inc(ht_done, 1)
                    elif kind == "z":
                        dd = slice(P * (x % 2), P * (x % 2) + P)
                        for k in range(CH):
                            pe.wait_ge(ht_lo_ready, nth(4, n, 2 * (x // 2) + k))
                            mm = three(bank[:, :], m_hi[:, k, dd], m_lo[:, k, dd],
                                       ht_hi[:, k, cols], ht_lo[:, k, cols], k == 0, k == CH - 1)
                        mm.then_inc(z_done, 1)
                    else:
                        pe.wait_ge(ht_lo_ready, nth(4, n, 2 * (x // QT) + 1))
                        rows_x = slice(P * x, P * x + P)
                        for k in range(CH):
                            mm = three(bank[:, 0:VW], ht_hi[:, k, rows_x], ht_lo[:, k, rows_x],
                                       wv_hi[:, k], wv_lo[:, k], k == 0, k == CH - 1)
                        mm.then_inc(v_done, 1)

                norm = norm_steps(i, s, layer1, layer0)
                side = side_steps(i, s, layer1, layer0)
                end = end_steps(i, s, layer1, layer0)
                end_before = end_steps(i, s - 1, layer1, layer0) if s else None
                late = (b - 1, TILES - 1) if s == 0 else (b, s - 1)
                has_late = before if s == 0 else layer1
                agg_of = (b, TILES - 1) if s == 0 else (a, s - 1)
                has_agg = layer1 if s == 0 else layer0
                if s == 4 and layer1:
                    if layer0:
                        pe.wait_ge(a_t_ready, nth(TILES, a, s - 1))
                    operation(("h", b, 2), bank_t)
                    pe.wait_ge(p_ready, nth(TILES, b, s - (1 if layer0 else 2)))
                    operation(("h", b, 3), bank_s)
                    values(b, s - 2, range(QT - 1, QT))
                    values(*late, range(QT - 2))
                    operation(("z", b, 2), bank_t)
                    operation(("z", b, 3), bank_s)
                    if has_agg:
                        aggregate(*agg_of, range(1))
                    pe.wait_ge(z_lo_ready, nth(4, b, 2))
                    operation(("v", b, 4), bank_t)
                    values(*late, range(QT - 2, QT - 1))
                    scores(s)
                    if has_agg:
                        aggregate(*agg_of, range(1, CH))
                    if layer0:
                        transposes()
                    values(*late, range(QT - 1, QT))
                    return
                if layer1 and (layer0 or s <= KT):
                    scores(s)
                if layer1 and not layer0 and KT <= s < TILES - 1:
                    scores(s + 1)
                if side and not first:
                    if s == 5 and not layer0:
                        pe.wait_ge(v_lo_ready, nth(KT, b, 4))
                    else:
                        bank_t_free_before()
                    operation(side, op_bank(side, first))
                if norm and not first:
                    y_pair(*norm)
                ahead = (QT if norm[2] == 0 else 1) if norm else 1 if s == 0 else 0
                behind = 1 if end and s > 11 or s == 3 else 0
                if first:
                    transposes()
                if norm and first:
                    y_pair(*norm)
                if side and first and s > 13:
                    pe.wait_ge(z_lo_ready, nth(4, side[1], s - 15))
                    operation(side, op_bank(side, first))
                if has_agg:
                    aggregate(*agg_of, range(CH))
                if side and first and s == 13:
                    operation(side, op_bank(side, first))
                if has_late and ahead:
                    values(*late, range(ahead))
                if layer0 and not first:
                    transposes()
                if has_late and ahead < QT:
                    values(*late, range(ahead, QT - behind))
                if end:
                    kind, n, x = end
                    if first and kind == "h":
                        pe.wait_ge(weights_ready, 1)
                    elif layer0 and not first:
                        pe.wait_ge(a_t_ready, nth(TILES, a, s))
                    elif kind == "v":
                        pe.wait_ge(v_lo_ready, nth(KT, n, x - 1))
                    operation(end, op_bank(end, first))
                    if has_late and behind:
                        values(*late, range(QT - behind, QT))
                if first and s == 4:
                    weight_products()

            turns(pe, step, setup)


_INS = ["x", "adj", "L0_gnn_W", "L0_gnn_b", "L1_gnn_Wq_w", "L1_gnn_Wq_b", "L1_gnn_Wk_w",
        "L1_gnn_Wk_b", "L1_gnn_Wv_w", "L1_gnn_Wv_b"]


def kernel(**inputs):
    import numpy as _np
    import concourse.bacc as _bacc
    from concourse.bass_utils import run_bass_kernel_spmd as _run

    nc = _bacc.Bacc("TRN2", target_bir_lowering=False, num_devices=1)
    arrays, args = {}, []
    for name in _INS:
        a = _np.ascontiguousarray(inputs[name])
        arrays[f"in_{name}_dram"] = a
        args.append(nc.dram_tensor(f"in_{name}_dram", a.shape, mybir.dt.from_np(a.dtype),
                                   kind="ExternalInput").ap())
    out = nc.dram_tensor("out_dram", inputs["x"].shape, F32, kind="ExternalOutput").ap()
    build(nc, *args, out)
    r = _run(nc, [arrays], core_ids=[0])
    return r.results[0]["out_dram"]
```
